# Optimizing a Trainium2 kernel written in Bass

```python
import numpy as np
import jax
import jax.numpy as jnp

def _softmax(x, axis=-1):
    return jax.nn.softmax(x, axis=axis)

def _gelu(x):
    return jax.nn.gelu(x, approximate=True)

def _silu(x):
    return jax.nn.silu(x)

def _sigmoid(x):
    return jax.nn.sigmoid(x)

def _layernorm(x, axis=-1, eps=1e-05):
    m = jnp.mean(x, axis=axis, keepdims=True)
    v = jnp.var(x, axis=axis, keepdims=True)
    return (x - m) / jnp.sqrt(v + eps)

def _scatter_add(tgt, idx, src, axis=0):
    return tgt.at[idx].add(src)

def _segment_sum(src, seg, n):
    return jax.ops.segment_sum(src, seg, n)
kernel_name = 'mk_adj_preln_d2_adj_r2_c015ac'

def setup_inputs(seed: int=0):
    np.random.seed(seed)
    _w = jnp.asarray

    def _rec_inputs():
        import jax
        import jax.numpy as jnp
        _gk = jax.random.key(seed)
        x = 7.22e-05 + 1 * jax.random.normal(jax.random.fold_in(_gk, 1), (64, 128, 512), jnp.float32)
        _w = (1.0 + jnp.arange(128, dtype=jnp.float32)) ** (-0.5)
        _w = _w / _w.mean()
        _pij = jnp.clip(0.015625 * _w[:, None] * _w[None, :], 0.0, 1.0)
        _a = jax.random.uniform(jax.random.fold_in(_gk, 2), (64, 128, 128)) < _pij
        _a = jnp.logical_or(_a, jnp.swapaxes(_a, -1, -2))
        _a = jnp.logical_or(_a, jnp.eye(128, dtype=bool))
        _af = _a.astype(jnp.float32)
        _af = _af * jax.random.uniform(jax.random.fold_in(_gk, 3), (64, 128, 128), jnp.float32, 0.05, 4.42607)
        adj = _af
        return (x, adj)
    x, adj = _rec_inputs()

    def _L0_gnn_setup():
        import jax, jax.numpy as jnp
        import numpy as np
        NUM_HEADS = 16
        key = jax.random.key(seed)
        ks = jax.random.split(key, 7)
        B, N, D = (16, 256, 512)
        return {'x': jax.random.normal(ks[0], (B, N, D), dtype=jnp.float32), 'spatial_encoding': jax.random.normal(ks[1], (B, N, N), dtype=jnp.float32), 'edge_encoding': jax.random.normal(ks[2], (B, N, N), dtype=jnp.float32), 'Wq': jax.random.normal(ks[3], (D, D), dtype=jnp.float32) * D ** (-0.5), 'Wk': jax.random.normal(ks[4], (D, D), dtype=jnp.float32) * D ** (-0.5), 'Wv': jax.random.normal(ks[5], (D, D), dtype=jnp.float32) * D ** (-0.5), 'Wo': jax.random.normal(ks[6], (D, D), dtype=jnp.float32) * D ** (-0.5)}
    _L0_gnn_all = _L0_gnn_setup()
    _L0_gnn_in = {k: v for k, v in _L0_gnn_all.items() if k in ('Wq', 'Wk', 'Wv', 'Wo')}
    del _L0_gnn_all

    def _L1_gnn_setup():
        import jax, jax.numpy as jnp
        import numpy as np
        B, N, H, E = (64, 256, 512, 4)
        BN_EPS = 1e-05
        key = jax.random.key(seed)
        ks = jax.random.split(key, 6)
        x = jax.random.normal(ks[0], (B, N, H), dtype=jnp.float32)
        adj = jax.random.uniform(ks[1], (B, N, N), dtype=jnp.float32)
        stdv = 1.0 / np.sqrt(H)
        expert_w = jax.random.uniform(ks[2], (E, H, H), minval=-stdv, maxval=stdv, dtype=jnp.float32)
        r_std = 1.0 / np.sqrt(H)
        router_w = jax.random.uniform(ks[3], (H, E), minval=-r_std, maxval=r_std, dtype=jnp.float32)
        router_b = jax.random.uniform(ks[4], (E,), minval=-r_std, maxval=r_std, dtype=jnp.float32)
        bn_gamma = jnp.ones((E, H), dtype=jnp.float32)
        bn_beta = jnp.zeros((E, H), dtype=jnp.float32)
        return {'x': x, 'adj': adj, 'router_w': router_w, 'router_b': router_b, 'expert_w': expert_w, 'bn_gamma': bn_gamma, 'bn_beta': bn_beta}
    _L1_gnn_all = _L1_gnn_setup()
    _L1_gnn_in = {k: v for k, v in _L1_gnn_all.items() if k in ('router_w', 'router_b', 'expert_w', 'bn_gamma', 'bn_beta')}
    del _L1_gnn_all
    return {'x': x, 'adj': adj, 'L0_gnn_Wq': _L0_gnn_in['Wq'], 'L0_gnn_Wk': _L0_gnn_in['Wk'], 'L0_gnn_Wv': _L0_gnn_in['Wv'], 'L0_gnn_Wo': _L0_gnn_in['Wo'], 'L1_gnn_router_w': _L1_gnn_in['router_w'], 'L1_gnn_router_b': _L1_gnn_in['router_b'], 'L1_gnn_expert_w': _L1_gnn_in['expert_w'], 'L1_gnn_bn_gamma': _L1_gnn_in['bn_gamma'], 'L1_gnn_bn_beta': _L1_gnn_in['bn_beta']}

def reference(x, adj, L0_gnn_Wq, L0_gnn_Wk, L0_gnn_Wv, L0_gnn_Wo, L1_gnn_router_w, L1_gnn_router_b, L1_gnn_expert_w, L1_gnn_bn_gamma, L1_gnn_bn_beta):
    import jax
    import jax.numpy as jnp

    def _L0_gnn_ref(x, spatial_encoding, edge_encoding, Wq, Wk, Wv, Wo):
        import jax, jax.numpy as jnp
        import numpy as np
        NUM_HEADS = 16
        B, N, D = x.shape
        H = NUM_HEADS
        hd = D // H
        scale = D ** (-0.5)

        def split_heads(t):
            return t.reshape(B, N, H, hd).transpose(0, 2, 1, 3)
        q = split_heads(x @ Wq.T)
        k = split_heads(x @ Wk.T)
        v = split_heads(x @ Wv.T)
        bias = (spatial_encoding + edge_encoding)[:, None]
        a = jnp.einsum('bhnd,bhmd->bhnm', q, k) * scale + bias
        row_nonzero = jnp.any(a != 0, axis=-1, keepdims=True)
        a = jnp.where(row_nonzero, a, -jnp.inf)
        p = jax.nn.softmax(a, axis=-1)
        p = jnp.where(jnp.isnan(p), 0.0, p)
        o = jnp.einsum('bhnm,bhmd->bhnd', p, v)
        o = o.transpose(0, 2, 1, 3).reshape(B, N, D)
        return o @ Wo.T

    def _L1_gnn_ref(x, adj, router_w, router_b, expert_w, bn_gamma, bn_beta):
        import jax, jax.numpy as jnp
        import numpy as np
        B, N, H, E = (64, 256, 512, 4)
        BN_EPS = 1e-05
        scores = x.mean(axis=1) @ router_w + router_b
        top1 = jnp.argmax(scores, axis=-1)
        n_exp = expert_w.shape[0]
        W = expert_w[top1]
        support = jnp.einsum('bnh,bhk->bnk', x, W)
        out = jnp.einsum('bnm,bmk->bnk', adj, support)
        s = jax.ops.segment_sum(out.sum(axis=1), top1, num_segments=n_exp)
        ss = jax.ops.segment_sum((out * out).sum(axis=1), top1, num_segments=n_exp)
        cnt = jax.ops.segment_sum(jnp.ones_like(top1, dtype=out.dtype), top1, num_segments=n_exp) * out.shape[1]
        cnt = jnp.maximum(cnt, 1.0)[:, None]
        mean = s / cnt
        var = ss / cnt - mean * mean
        m = mean[top1][:, None, :]
        inv = jax.lax.rsqrt(var[top1][:, None, :] + BN_EPS)
        y = (out - m) * inv * bn_gamma[top1][:, None, :] + bn_beta[top1][:, None, :]
        return jax.nn.relu(y)
    h = jnp.maximum(_layernorm(x, axis=-1), 0.0)
    x = x + _L0_gnn_ref(h, adj, adj, L0_gnn_Wq, L0_gnn_Wk, L0_gnn_Wv, L0_gnn_Wo)
    h = jnp.maximum(_layernorm(x, axis=-1), 0.0)
    x = x + _L1_gnn_ref(h, adj, L1_gnn_router_w, L1_gnn_router_b, L1_gnn_expert_w, L1_gnn_bn_gamma, L1_gnn_bn_beta)
    return x

_drawn_inputs = setup_inputs


def setup_inputs(seed=0):
    import zlib

    import numpy as np

    out = dict(_drawn_inputs(seed))
    spreads = {'L1_gnn_bn_gamma': (1.0, 0.2), 'L1_gnn_bn_beta': (0.0, 0.1)}
    factors = {'L0_gnn_Wq': 3.431, 'L0_gnn_Wk': 3.379}
    for name, (base, spread) in spreads.items():
        noise = np.random.default_rng([zlib.crc32(name.encode()), seed]).standard_normal(out[name].shape)
        drawn = base * np.exp(spread * noise) if base else spread * noise
        out[name] = jnp.asarray(drawn.astype(out[name].dtype))
    for name, factor in factors.items():
        out[name] = (out[name] * factor).astype(out[name].dtype)
    return out
```

```python
from contextlib import ExitStack

import concourse.bass as bass
from concourse import mybir

F32 = mybir.dt.float32
F32R = mybir.dt.float32r
I32 = mybir.dt.int32
ALU = mybir.AluOpType
ACT = mybir.ActivationFunctionType
X = mybir.AxisListType.X

HEADS = 16
EPS = 1e-5


def wait(engine, semaphore, value):
    if not isinstance(value, int) or value > 0:
        engine.wait_ge(semaphore, value)


def exact_product(nc, out, a_hi, a_lo, b_hi, b_lo):
    terms = [t for k in range(len(a_hi)) for t in ((a_hi[k], b_hi[k]), (a_hi[k], b_lo[k]), (a_lo[k], b_hi[k]))]
    for n, (a, b) in enumerate(terms):
        last = nc.tensor.matmul(out, a, b, start=(n == 0), stop=(n == len(terms) - 1))
    return last


def halves_combined(nc, bn, mean_sum, mean_diff, m2):
    nc.vector.tensor_tensor(mean_sum[:], bn[:, :, 1], bn[:, :, 4], ALU.add)
    nc.vector.tensor_tensor(mean_diff[:], bn[:, :, 1], bn[:, :, 4], ALU.subtract)
    return nc.vector.tensor_tensor(m2[:], bn[:, :, 2], bn[:, :, 5], ALU.add)


def scaled_moments(nc, count, mean_sum, mean_diff, m2, neg_mean):
    nc.vector.tensor_scalar(neg_mean[:], mean_sum[:], -0.5, None, ALU.mult)
    nc.vector.tensor_tensor(mean_diff[:], mean_diff[:], mean_diff[:], ALU.mult)
    return nc.vector.tensor_scalar(m2[:], m2[:], 1.0 / count, EPS, ALU.mult, ALU.add)


def attention_layer(nc, ctx, sem, ident, x, adj, weights, x1_dram):
    B, N, D = x.shape
    PAIRS = B // 2
    KC = D // 128
    R = 4
    C = HEADS // R
    HD = D // HEADS
    STEPS = 2 * C
    SCALE = float(D) ** -0.5
    STACKS = 16 * 3 * R

    def sb(name, shape, dt=F32):
        return ctx.enter_context(nc.sbuf_tensor(name, shape, dt))

    def ps(name, shape):
        return ctx.enter_context(nc.psum_tensor(name, shape, F32))

    w_hi = sb("w_hi", [N, 4, KC, D], F32R)
    w_lo = sb("w_lo", [N, 4, KC, D], F32R)
    x_in = sb("x_in", [N, 2, D])
    h = sb("h", [N, 2, D])
    hT_hi = sb("hT_hi", [128, KC, 2, N], F32R)
    hT_lo = sb("hT_lo", [128, KC, 2, N], F32R)
    Q_LO, Q_HI, K_HI, K_LO = range(4)
    qk = sb("qk", [128, 4, 2, C, N], F32R)
    stack = sb("stack", [3 * HD, 2, R, 2, C, N], F32R)
    v = sb("v", [N, 2, D])
    logits = sb("logits", [N, 4, R, N])
    prob = sb("prob", [N, 4, R, N])
    probT = sb("probT", [N, 4, R, N])
    o_hi = sb("o_hi", [128, C, N], F32R)
    o_lo = sb("o_lo", [128, C, N], F32R)
    x_res = sb("x_res", [N, 2, D])
    adj_in = sb("adj_in", [N, 2, N])
    adj2 = sb("adj2", [N, 2, N])
    bn = sb("bn", [N, 2, 6])
    mean_sum = sb("mean_sum", [N, 2])
    mean_diff = sb("mean_diff", [N, 2])
    m2 = sb("m2", [N, 2])
    var_eps = sb("var_eps", [N, 2])
    neg_mean = sb("neg_mean", [N, 2])
    minus_half = sb("minus_half", [N, 2])
    rstd = sb("rstd", [N, 2])
    shift = sb("shift", [N, 2])
    neg_max = sb("neg_max", [N, 4, R])
    abs_max = sb("abs_max", [N, 4, R])
    row_sum = sb("row_sum", [N, 4, R])
    inv_sum = sb("inv_sum", [N, 4, R])
    norm = sb("norm", [N, 4, R])

    scores_ps = ps("scores_ps", [N, 2, R, N])
    probT_ps = ps("probT_ps", [N, 2, R, N])
    o_ps = ps("o_ps", [128, C, N])
    bank = ps("bank", [128, 3, 512])

    w_loaded, w_hi_ready, w_split = sem("w_loaded"), sem("w_hi_ready"), sem("w_split")
    x_loaded, var_ready, rstd_ready, shift_ready, h_ready = map(
        sem, ("x_loaded", "var_ready", "rstd_ready", "shift_ready", "h_ready"))
    bn_done, halves_done, scaled_done = sem("bn_done"), sem("halves_done"), sem("scaled_done")
    h_transposed, hT_hi_ready, hT_split = sem("h_transposed"), sem("hT_hi_ready"), sem("hT_split")
    qk_projected, qk_hi_ready, qk_split = sem("qk_projected"), sem("qk_hi_ready"), sem("qk_split")
    stacked = [sem("stacked0"), sem("stacked1")]
    v_projected, v_copied = sem("v_projected"), sem("v_copied")
    adj_loaded, adj_doubled = sem("adj_loaded"), sem("adj_doubled")
    scored, logits_ready, neg_max_ready, abs_max_ready = map(
        sem, ("scored", "logits_ready", "neg_max_ready", "abs_max_ready"))
    exp_done, inverted, norm_ready, normed = map(sem, ("exp_done", "inverted", "norm_ready", "normed"))
    transposed, probT_ready, applied = sem("transposed"), sem("probT_ready"), sem("applied")
    o_hi_ready, o_split, o_projected = sem("o_hi_ready"), sem("o_split"), sem("o_projected")
    x_res_loaded = [sem("x_res_loaded0"), sem("x_res_loaded1")]
    x1_ready = sem("x1_ready")
    x1_stored = [sem("x1_stored0"), sem("x1_stored1")]
    half_ready = sem("half_ready")

    PE_ORDER = "S0 S1 Q0 S2 Q1 T0 S3 Q2 T1 W0 S4 Q3 T2 W1 S5 T3 W2 S6 V0 W3 T4 S7 O0 T5 W4 V1 T6 W5 H0 T7 W6 H1 W7 O1"
    ACT_ORDER = "E0 Q0 E1 C0 Q1 E2 C1 Q2 E3 C2 Q3 E4 C3 E5 O0 V0 C4 A0 A1 E6 C5 E7 H0 C6 H1 C7 V1 O1"
    DVE_ORDER = "L0 L1 Q0 L2 R0 Q1 L3 R1 Q2 L4 R2 Q3 L5 R3 N L6 R4 O0 L7 R5 X0 R6 H0 R7 H1 O1 X1"
    POOL_ORDER = "P0 P1 P2 P3 G P4 P5 P6 D P7"

    def tokens(order, attend, project, normalise):
        on = {}
        on.update(dict.fromkeys("STWOECLRPX", attend))
        on.update(dict.fromkeys("QVD", project))
        on.update(dict.fromkeys("HANG", normalise))
        return [(t[0], int(t[1:] or 0)) for t in order.split() if on[t[0]]]

    def run(engine, body):
        body(-2, False, False, True)
        body(-1, False, True, True)
        body(0, True, True, True)
        with engine.Fori(1, PAIRS - 2) as i:
            body(i, True, True, True)
        body(PAIRS - 2, True, True, False)
        body(PAIRS - 1, True, False, False)

    with nc.Block() as block:

        @block.sync
        def _(sp):
            for n, w in enumerate(weights):
                raw = (logits, prob, probT)[n % 3]
                if n >= 3:
                    sp.wait_ge(w_split, n - 2)
                sp.dma_start(raw[:].rearrange("p k r n -> p k (r n)"),
                             w.rearrange("(k p) f -> p k f", p=128)).then_inc(w_loaded, 16)
                if n == 0:
                    sp.dma_start(x_in[:], x[0:2].rearrange("g n f -> n g f")).then_inc(x_loaded, 16)
                sp.wait_ge(w_loaded, 16 * (n + 1))

            def body(i, attend, project, normalise):
                if normalise and not (isinstance(i, int) and i == -2):
                    wait(sp, h_ready, 2 * (i + 2))
                    sp.dma_start(x_in[:], x[bass.ds(2 * (i + 2), 2)].rearrange("g n f -> n g f")).then_inc(x_loaded, 16)
                if project:
                    wait(sp, adj_doubled, i + 1)
                    sp.dma_start(adj_in[:], adj[bass.ds(2 * (i + 1), 2)].rearrange("g n m -> n g m")).then_inc(adj_loaded, 16)
                if attend:
                    for g in range(2):
                        wait(sp, x1_stored[g], 16 * i)
                        sp.dma_start(x_res[:, g, :], x[bass.ds(2 * i + g, 1)].rearrange("g n f -> n (g f)")).then_inc(x_res_loaded[g], 16)
                if project:
                    wait(sp, qk_split, 4 * (i + 2))
                    for g in range(2):
                        if attend:
                            wait(sp, scored, STEPS * i + C * (g + 1))
                        for s, (a, b) in enumerate(((Q_HI, K_HI), (Q_LO, K_HI), (Q_HI, K_LO))):
                            for r in range(R):
                                sp.dma_start(
                                    stack[HD * s:HD * s + HD, g, r].bitcast(F32).rearrange("p t c n -> p t (c n)"),
                                    qk[HD * r:HD * r + HD, a:b + 1:b - a, g].bitcast(F32).rearrange("p t c n -> p t (c n)"),
                                ).then_inc(stacked[g], 16)
                if attend:
                    for g in range(2):
                        wait(sp, x1_ready, 2 * i + g + 1)
                        sp.dma_start(x1_dram[bass.ds(2 * i + g, 1)].rearrange("g n f -> n (g f)"), x_res[:, g, :]).then_inc(x1_stored[g], 16)

            run(sp, body)
            for g in range(2):
                sp.wait_ge(x1_stored[g], 16 * PAIRS)

        @block.gpsimd
        def _(pool):
            nc.gpsimd.memset(minus_half[:], -0.5).then_inc(half_ready, 1)
            pool.wait_ge(half_ready, 1)

            def body(i, attend, project, normalise):
                for token, k in tokens(POOL_ORDER, attend, project, normalise):
                    if token == "P":
                        slot = k % 4
                        wait(pool, norm_ready, STEPS * i + k + 1)
                        nc.gpsimd.tensor_tensor(prob[:, slot], prob[:, slot],
                                                norm[:, slot].unsqueeze(2).to_broadcast([N, R, N]),
                                                ALU.mult).then_inc(normed, 1)
                    elif token == "G":
                        wait(pool, var_ready, i + 3)
                        wait(pool, h_ready, 2 * (i + 2))
                        nc.gpsimd.tensor_tensor(rstd[:], var_eps[:], minus_half[:], ALU.pow).then_inc(rstd_ready, 1)
                        wait(pool, rstd_ready, i + 3)
                        nc.gpsimd.tensor_tensor(shift[:], neg_mean[:], rstd[:], ALU.mult).then_inc(shift_ready, 1)
                    elif token == "D":
                        wait(pool, adj_loaded, 16 * (i + 2))
                        if attend:
                            wait(pool, logits_ready, STEPS * (i + 1))
                        nc.gpsimd.tensor_tensor(adj2[:], adj_in[:], adj_in[:], ALU.add).then_inc(adj_doubled, 1)

            run(pool, body)

        @block.scalar
        def _(act):
            for n in range(4):
                act.wait_ge(w_loaded, 16 * (n + 1))
                raw = (logits, prob, probT)[n % 3]
                nc.scalar.activation(w_hi[:, n], raw[:].rearrange("p k r n -> p k (r n)"), ACT.Copy).then_inc(w_hi_ready, 1)

            def body(i, attend, project, normalise):
                for token, k in tokens(ACT_ORDER, attend, project, normalise):
                    slot = k % 4
                    if token == "E":
                        wait(act, neg_max_ready, STEPS * i + k + 1)
                        wait(act, transposed, STEPS * i + k - 3)
                        for r in range(R):
                            last = nc.scalar.activation(prob[:, slot, r], logits[:, slot, r], ACT.Exp,
                                                        bias=neg_max[:, slot, r:r + 1],
                                                        accum_out=row_sum[:, slot, r:r + 1])
                        last.then_inc(exp_done, 1)
                    elif token == "C":
                        wait(act, transposed, STEPS * i + k + 1)
                        wait(act, applied, STEPS * i + k - 3)
                        nc.scalar.activation(probT[:, slot], probT_ps[:, k % 2], ACT.Copy).then_inc(probT_ready, 1)
                    elif token == "O":
                        wait(act, applied, STEPS * i + C * (k + 1))
                        wait(act, o_projected, 2 * i + k)
                        nc.scalar.activation(o_hi[:], o_ps[:], ACT.Copy).then_inc(o_hi_ready, 1)
                    elif token == "Q":
                        wait(act, qk_projected, 4 * (i + 1) + k + 1)
                        if k == 0:
                            for g in range(2):
                                wait(act, stacked[g], STACKS * (i + 1))
                        t, c = (Q_HI, K_HI)[k // 2], 2 * (k % 2)
                        nc.scalar.activation(qk[:, t, :, c:c + 2].rearrange("p g c n -> p c g n"),
                                             bank[:, (0, 1, 2, 0)[k]].rearrange("p (c g n) -> p c g n", c=2, g=2),
                                             ACT.Copy).then_inc(qk_hi_ready, 1)
                    elif token == "V":
                        wait(act, v_projected, 2 * (i + 1) + k + 1)
                        if attend:
                            wait(act, applied, STEPS * i + C * (k + 1))
                        nc.scalar.activation(v[:, k], bank[:, (1, 0)[k]], ACT.Copy).then_inc(v_copied, 1)
                    elif token == "A":
                        wait(act, shift_ready, i + 3)
                        wait(act, h_transposed, 2 * (i + 2))
                        nc.scalar.activation(h[:, k], x_in[:, k], ACT.Relu, bias=shift[:, k:k + 1],
                                             scale=rstd[:, k:k + 1]).then_inc(h_ready, 1)
                    elif token == "H":
                        wait(act, h_transposed, 2 * (i + 2) + k + 1)
                        nc.scalar.activation(hT_hi[:, :, k], bank[:, 1 + k].rearrange("p (c n) -> p c n", n=N),
                                             ACT.Copy).then_inc(hT_hi_ready, 1)

            run(act, body)

        @block.vector
        def _(dve):
            for n in range(4):
                dve.wait_ge(w_hi_ready, n + 1)
                raw = (logits, prob, probT)[n % 3]
                nc.vector.tensor_tensor(w_lo[:, n], raw[:].rearrange("p k r n -> p k (r n)"), w_hi[:, n],
                                        ALU.subtract).then_inc(w_split, 1)

            def body(i, attend, project, normalise):
                for token, k in tokens(DVE_ORDER, attend, project, normalise):
                    slot = k % 4
                    if token == "L":
                        wait(dve, scored, STEPS * i + k + 1)
                        wait(dve, exp_done, STEPS * i + k - 3)
                        if k == 0:
                            wait(dve, adj_doubled, i + 1)
                            if isinstance(i, int) and i == 0:
                                dve.wait_ge(w_split, 4)
                        nc.vector.scalar_tensor_tensor(
                            out=logits[:, slot], in0=scores_ps[:, k % 2], scalar=SCALE,
                            in1=adj2[:, k // C].unsqueeze(1).to_broadcast([N, R, N]),
                            op0=ALU.mult, op1=ALU.add).then_inc(logits_ready, 1)
                        wait(dve, logits_ready, STEPS * i + k + 1)
                        nc.vector.tensor_reduce(neg_max[:, slot], logits[:, slot], X, ALU.max,
                                                negate=True).then_inc(neg_max_ready, 1)
                        nc.vector.tensor_reduce(abs_max[:, slot], logits[:, slot], X, ALU.max,
                                                apply_absolute_value=True).then_inc(abs_max_ready, 1)
                    elif token == "R":
                        wait(dve, exp_done, STEPS * i + k + 1)
                        wait(dve, abs_max_ready, STEPS * i + k + 1)
                        nc.vector.reciprocal(inv_sum[:, slot], row_sum[:, slot]).then_inc(inverted, 1)
                        wait(dve, inverted, STEPS * i + k + 1)
                        wait(dve, normed, STEPS * i + k - 3)
                        nc.vector.scalar_tensor_tensor(
                            out=norm[:, slot], in0=abs_max[:, slot], scalar=0.0, in1=inv_sum[:, slot],
                            op0=ALU.not_equal, op1=ALU.mult).then_inc(norm_ready, 1)
                    elif token == "O":
                        wait(dve, o_hi_ready, 2 * i + k + 1)
                        nc.vector.tensor_tensor(o_lo[:], o_ps[:], o_hi[:], ALU.subtract).then_inc(o_split, 1)
                    elif token == "X":
                        wait(dve, o_projected, 2 * i + k + 1)
                        wait(dve, x_res_loaded[k], 16 * (i + 1))
                        nc.vector.tensor_tensor(x_res[:, k], bank[:, (2, 1)[k]], x_res[:, k],
                                                ALU.add).then_inc(x1_ready, 1)
                    elif token == "Q":
                        wait(dve, qk_hi_ready, 4 * (i + 1) + k + 1)
                        hi, lo = ((Q_HI, Q_LO), (K_HI, K_LO))[k // 2]
                        c = 2 * (k % 2)
                        nc.vector.tensor_tensor(qk[:, lo, :, c:c + 2].rearrange("p g c n -> p c g n"),
                                                bank[:, (0, 1, 2, 0)[k]].rearrange("p (c g n) -> p c g n", c=2, g=2),
                                                qk[:, hi, :, c:c + 2].rearrange("p g c n -> p c g n"),
                                                ALU.subtract).then_inc(qk_split, 1)
                    elif token == "N":
                        wait(dve, x_loaded, 16 * (i + 3))
                        for g in range(2):
                            last = nc.vector.bn_stats(bn[:, g], x_in[:, g])
                        last.then_inc(bn_done, 1)
                        wait(dve, bn_done, i + 3)
                        halves_combined(nc, bn, mean_sum, mean_diff, m2).then_inc(halves_done, 1)
                        wait(dve, halves_done, i + 3)
                        wait(dve, shift_ready, i + 2)
                        scaled_moments(nc, D, mean_sum, mean_diff, m2, neg_mean).then_inc(scaled_done, 1)
                        wait(dve, scaled_done, i + 3)
                        nc.vector.scalar_tensor_tensor(out=var_eps[:], in0=mean_diff[:], scalar=0.25, in1=m2[:],
                                                       op0=ALU.mult, op1=ALU.add).then_inc(var_ready, 1)
                    elif token == "H":
                        wait(dve, hT_hi_ready, 2 * (i + 2) + k + 1)
                        nc.vector.tensor_tensor(hT_lo[:, :, k], bank[:, 1 + k].rearrange("p (c n) -> p c n", n=N),
                                                hT_hi[:, :, k], ALU.subtract).then_inc(hT_split, 1)

            run(dve, body)

        @block.tensor
        def _(pe):
            def body(i, attend, project, normalise):
                for token, k in tokens(PE_ORDER, attend, project, normalise):
                    g, c, slot = k // C, k % C, k % 4
                    if token == "S":
                        if c == 0:
                            wait(pe, stacked[g], STACKS * (i + 1))
                        wait(pe, logits_ready, STEPS * i + k - 1)
                        for r in range(R):
                            last = nc.tensor.matmul(scores_ps[:, k % 2, r], stack[:, g, r, 0, c], stack[:, g, r, 1, c],
                                                    start=True, stop=True)
                        last.then_inc(scored, 1)
                    elif token == "T":
                        wait(pe, normed, STEPS * i + k + 1)
                        wait(pe, probT_ready, STEPS * i + k - 1)
                        for r in range(R):
                            last = nc.tensor.transpose(probT_ps[:, k % 2, r], prob[:, slot, r], ident[:])
                        last.then_inc(transposed, 1)
                    elif token == "W":
                        wait(pe, probT_ready, STEPS * i + k + 1)
                        if c == 0:
                            wait(pe, v_copied, 2 * i + g + 1)
                            wait(pe, o_split, 2 * i + g)
                        for r in range(R):
                            f = HD * (R * c + r)
                            last = nc.tensor.matmul(o_ps[HD * r:HD * r + HD, c], v[:, g, f:f + HD], probT[:, slot, r],
                                                    start=True, stop=True)
                        last.then_inc(applied, 1)
                    elif token == "O":
                        wait(pe, o_split, 2 * i + k + 1)
                        if k == 0 and project:
                            wait(pe, qk_split, 4 * (i + 1) + 3)
                        if not project:
                            wait(pe, x1_ready, 2 * i)
                        if k == 1 and normalise:
                            wait(pe, hT_split, 2 * (i + 2) + 1)
                        if k == 1 and project and not normalise:
                            wait(pe, v_copied, 2 * (i + 1) + 1)
                        exact_product(nc, bank[:, (2, 1)[k]], [o_hi[:, c] for c in range(C)], [o_lo[:, c] for c in range(C)],
                                      [w_hi[:, 3, c] for c in range(C)], [w_lo[:, 3, c] for c in range(C)]
                                      ).then_inc(o_projected, 1)
                    elif token == "Q":
                        if isinstance(i, int) and i == -1 and k % 2 == 0:
                            pe.wait_ge(w_split, k // 2 + 1)
                        if k == 0:
                            wait(pe, hT_split, 2 * (i + 2))
                        if k == 0:
                            wait(pe, v_copied, 2 * (i + 1))
                        if k == 1:
                            wait(pe, x1_ready, 2 * i)
                        if k == 3:
                            wait(pe, qk_split, 4 * (i + 1) + 1)
                        for j in range(2):
                            m = 128 * (2 * (k % 2) + j)
                            last = exact_product(nc, bank[:, (0, 1, 2, 0)[k], 256 * j:256 * j + 256],
                                                 [w_hi[:, k // 2, kc, m:m + 128] for kc in range(KC)],
                                                 [w_lo[:, k // 2, kc, m:m + 128] for kc in range(KC)],
                                                 [hT_hi[:, kc] for kc in range(KC)], [hT_lo[:, kc] for kc in range(KC)])
                        last.then_inc(qk_projected, 1)
                    elif token == "V":
                        if isinstance(i, int) and i == -1 and k == 0:
                            pe.wait_ge(w_split, 4)
                        wait(pe, qk_split, 4 * (i + 1) + (2, 4)[k])
                        exact_product(nc, bank[:, (1, 0)[k]], [hT_hi[:, kc, k] for kc in range(KC)],
                                      [hT_lo[:, kc, k] for kc in range(KC)],
                                      [w_hi[:, 2, kc] for kc in range(KC)], [w_lo[:, 2, kc] for kc in range(KC)]
                                      ).then_inc(v_projected, 1)
                    elif token == "H":
                        wait(pe, h_ready, 2 * (i + 2) + k + 1)
                        wait(pe, *((v_copied, 2 * (i + 1) + 1), (x1_ready, 2 * i + 1))[k])
                        for kc in range(KC):
                            last = nc.tensor.transpose(bank[:, 1 + k, 128 * kc:128 * kc + 128],
                                                       h[:, k, 128 * kc:128 * kc + 128], ident[:])
                        last.then_inc(h_transposed, 1)

            run(pe, body)


def expert_layer(nc, ctx, sem, ident, x1_dram, adj, router_w, router_b, expert_w, gamma, beta, out_dram, y):
    B, N, D = x1_dram.shape
    E = expert_w.shape[0]
    KC = D // 128
    G = 4
    GROUPS = B // G
    SLOTS = 2 * G

    def sb(name, shape, dt=F32):
        return ctx.enter_context(nc.sbuf_tensor(name, shape, dt))

    def ps(name, shape):
        return ctx.enter_context(nc.psum_tensor(name, shape, F32))

    ew_raw = sb("ew_raw", [128, 2, KC, D])
    ew_hi = sb("ew_hi", [128, E, KC, D], F32R)
    ew_lo = sb("ew_lo", [128, E, KC, D], F32R)
    x1_in = sb("x1_in", [N, SLOTS, D])
    h2 = x1_in[:, G:]
    out_sb = sb("out_sb", [N, SLOTS, D])
    square = out_sb[:, G:]
    adj_in2 = sb("adj_in2", [N, G, N])
    adjT = sb("adjT", [N, G, N + 1])
    z_hi = sb("z_hi", [128, G, KC, N], F32R)
    z_lo = sb("z_lo", [128, G, KC, N], F32R)
    mean_h = sb("mean_h", [128, G, KC])
    sums = sb("sums", [N, 2, E, D])
    rw = sb("rw", [128, KC, E])
    rb = sb("rb", [1, E])
    expert_less_e = sb("expert_less_e", [1, E])
    score = sb("score", [1, G, E])
    score_max = sb("score_max", [1, G])
    best = sb("best", [1, G, E])
    candidate = sb("candidate", [1, G, E])
    first = sb("first", [1, G])
    top1 = sb("top1", [1, B], I32)
    bn = sb("bn2", [N, G, 6])
    mean_sum = sb("mean_sum2", [N, G])
    mean_diff = sb("mean_diff2", [N, G])
    m2 = sb("m22", [N, G])
    var_eps = sb("var_eps2", [N, G])
    neg_mean = sb("neg_mean2", [N, G])
    minus_half = sb("minus_half2", [N, E * KC])
    rstd = sb("rstd2", [N, G])
    shift = sb("shift2", [N, G])
    ones = sb("ones", [N, 128])
    gamma_sb = sb("gamma_sb", [128, E, KC])
    beta_sb = sb("beta_sb", [128, E, KC])
    is_expert = sb("is_expert", [1, E, B])
    count = sb("count", [1, E])
    inv_count1 = sb("inv_count1", [1, E])
    inv_count = sb("inv_count", [128, E])
    moment = sb("moment", [128, 2, E, KC])
    mean_sq = sb("mean_sq", [128, E, KC])
    var = sb("var", [128, E, KC])
    inv_std = sb("inv_std", [128, E, KC])
    coef = sb("coef", [128, 2, E, KC])
    coef_rows = sb("coef_rows", [N, 2, E, D])

    adjT_ps = ps("adjT_ps", [N, G, N])
    router_ps = ps("router_ps", [128, 512])
    z_ps = ps("z_ps", [128, 2, 2, 512])
    out_ps = ps("out_ps", [N, 2, D])

    const_loaded, ew_loaded, ew_hi_ready, ew_split = map(sem, ("const_loaded", "ew_loaded", "ew_hi_ready", "ew_split"))
    consts = sem("consts")
    x1_loaded, adj2_loaded = sem("x1_loaded"), sem("adj2_loaded")
    bn_done, halves_done, scaled_done, var_ready, rstd_ready, shift_ready, h2_ready = map(
        sem, ("bn_done2", "halves_done2", "scaled_done2", "var_ready2", "rstd_ready2", "shift_ready2", "h2_ready"))
    adj_transposed, adjT_ready = sem("adj_transposed"), sem("adjT_ready")
    z_made, z_hi_ready, mean_ready, z_split = map(sem, ("z_made", "z_hi_ready", "mean_ready", "z_split"))
    router_scored, router_step, first_ready, routed = map(sem, ("router_scored", "router_step", "first_ready", "routed"))
    out_made, out_copied, squared, summed = map(sem, ("out_made", "out_copied", "squared", "summed"))
    out_stored = [sem(f"out_stored{g}") for g in range(G)]
    counted, count_ready, moments_made, moment_step = map(sem, ("counted", "count_ready", "moments_made", "moment_step"))
    var_all_ready, inv_std_ready, coef_ready, rows_made, rows_ready = map(
        sem, ("var_all_ready", "inv_std_ready", "coef_ready", "rows_made", "rows_ready"))
    slot_loaded = [sem(f"slot_loaded{s}") for s in range(SLOTS)]
    y_stored = [sem(f"y_stored{s}") for s in range(SLOTS)]
    scaled, shifted, y_ready = sem("scaled"), sem("shifted"), sem("y_ready")

    PE_ORDER = "P0 J P1 Z0 P2 Z1 P3 Z2 Z3 M"
    ACT_ORDER = "A0 A1 P0 A2 A3 P1 Z0 P2 Z1 P3 Z2 Z3"
    DVE_ORDER = "N J Z0 Z1 Z2 Z3 M"

    def tokens(order, mix, expert):
        on = {**dict.fromkeys("JZMAN", mix), "P": expert}
        return [(t[0], int(t[1:] or 0)) for t in order.split() if on[t[0]]]

    def run(engine, body):
        body(0, True, False)
        body(1, True, True)
        with engine.Fori(2, GROUPS) as i:
            body(i, True, True)
        body(GROUPS, False, True)

    with nc.Block() as block:

        @block.sync
        def _(sp):
            sp.dma_start(rw[:], router_w).then_inc(const_loaded, 16)
            sp.dma_start(rb[:], router_b).then_inc(const_loaded, 16)
            sp.dma_start(gamma_sb[:], gamma).then_inc(const_loaded, 16)
            sp.dma_start(beta_sb[:], beta).then_inc(const_loaded, 16)

            def load(i):
                wait(sp, h2_ready, G * i)
                sp.dma_start(x1_in[:, 0:G], x1_dram[bass.ds(G * i, G)].rearrange("g n f -> n g f")).then_inc(x1_loaded, 16)
                wait(sp, adj_transposed, i)
                sp.dma_start(adj_in2[:], adj[bass.ds(G * i, G)].rearrange("g n m -> n g m")).then_inc(adj2_loaded, 16)

            load(0)
            for e in range(E):
                if e >= 2:
                    sp.wait_ge(ew_split, e - 1)
                if e:
                    sp.wait_ge(ew_loaded, 16 * e)
                sp.dma_start(ew_raw[:, e % 2], expert_w[e].rearrange("(k p) f -> p k f", p=128)).then_inc(ew_loaded, 16)

            def body(i, mix, expert):
                if mix and not (isinstance(i, int) and i == 0):
                    load(i)
                if expert:
                    for g in range(G):
                        wait(sp, out_copied, G * (i - 1) + g + 1)
                        sp.dma_start(out_dram[bass.ds(G * (i - 1) + g, 1)].rearrange("g n f -> n (g f)"), out_sb[:, g]).then_inc(out_stored[g], 16)

            run(sp, body)
            for g in range(G):
                sp.wait_ge(out_stored[g], 16 * GROUPS)
            sp.wait_ge(summed, B)

            def load_slots(j):
                for s in range(SLOTS):
                    wait(sp, y_stored[s], 16 * j)
                    for src, dst in ((out_dram, out_sb), (x1_dram, x1_in)):
                        sp.dma_start(dst[:, s], src[bass.ds(SLOTS * j + s, 1)].rearrange("g n f -> n (g f)")).then_inc(slot_loaded[s], 16)

            load_slots(0)
            with sp.Fori(1, B // SLOTS) as j:
                load_slots(j)
            for s in range(SLOTS):
                sp.wait_ge(y_stored[s], 16 * (B // SLOTS))

        @block.gpsimd
        def _(pool):
            nc.gpsimd.memset(minus_half[:], -0.5)
            nc.gpsimd.memset(ones[:], 1.0)
            nc.gpsimd.memset(sums[:], 0.0)
            for e in range(E):
                nc.gpsimd.memset(expert_less_e[:, e:e + 1], float(e - E))
            nc.gpsimd.memset(adjT[:, :, N:N + 1], 1.0 / N).then_inc(consts, 1)
            pool.wait_ge(consts, 1)

            def body(i, mix, expert):
                if mix:
                    wait(pool, var_ready, i + 1)
                    wait(pool, h2_ready, G * i)
                    nc.gpsimd.tensor_tensor(rstd[:], var_eps[:], minus_half[:, 0:G], ALU.pow).then_inc(rstd_ready, 1)
                    wait(pool, rstd_ready, i + 1)
                    nc.gpsimd.tensor_tensor(shift[:], neg_mean[:], rstd[:], ALU.mult).then_inc(shift_ready, 1)
                if expert:
                    wait(pool, routed, i)
                    for g in range(G):
                        n = G * (i - 1) + g
                        e = pool.value_load(top1[0:1, bass.ds(n, 1)], min_val=0, max_val=E - 1)
                        wait(pool, squared, n + 1)
                        wait(pool, summed, n)
                        for t, src in enumerate((out_sb[:, g], square[:, g])):
                            total = sums[:, t, bass.ds(e, 1)].rearrange("p a f -> p (a f)")
                            last = nc.gpsimd.tensor_tensor(total, total, src, ALU.add)
                        last.then_inc(summed, 1)

            run(pool, body)
            pool.wait_ge(var_all_ready, 1)
            nc.gpsimd.tensor_tensor(inv_std[:].rearrange("p e c -> p (e c)"), var[:].rearrange("p e c -> p (e c)"),
                                    minus_half[:], ALU.pow).then_inc(inv_std_ready, 1)
            pool.wait_ge(rows_ready, 2 * E)
            with pool.Fori(0, B // SLOTS) as j:
                for s in range(SLOTS):
                    n = SLOTS * j + s
                    e = pool.value_load(top1[0:1, bass.ds(n, 1)], min_val=0, max_val=E - 1)
                    pool.wait_ge(scaled, n + 1)
                    nc.gpsimd.tensor_tensor(out_sb[:, s], out_sb[:, s],
                                            coef_rows[:, 1, bass.ds(e, 1)].rearrange("p a f -> p (a f)"),
                                            ALU.add).then_inc(shifted, 1)

        @block.scalar
        def _(act):
            for e in range(E):
                act.wait_ge(ew_loaded, 16 * (e + 1))
                nc.scalar.activation(ew_hi[:, e], ew_raw[:, e % 2], ACT.Copy).then_inc(ew_hi_ready, 1)

            def body(i, mix, expert):
                for token, g in tokens(ACT_ORDER, mix, expert):
                    if token == "A":
                        wait(act, shift_ready, i + 1)
                        wait(act, z_made, G * (i - 1) + g + 1)
                        nc.scalar.activation(h2[:, g], x1_in[:, g], ACT.Relu, bias=shift[:, g:g + 1],
                                             scale=rstd[:, g:g + 1]).then_inc(h2_ready, 1)
                    elif token == "P":
                        n = G * (i - 1) + g
                        wait(act, out_made, n + 1)
                        wait(act, out_stored[g], 16 * (i - 1))
                        wait(act, summed, n - G + 1)
                        nc.scalar.activation(out_sb[:, g], out_ps[:, g % 2], ACT.Copy).then_inc(out_copied, 1)
                        nc.scalar.activation(square[:, g], out_ps[:, g % 2], ACT.Square).then_inc(squared, 1)
                    elif token == "Z":
                        n = G * i + g
                        wait(act, z_made, n + 1)
                        wait(act, out_made, n - G + 1)
                        nc.scalar.activation(z_hi[:, g].rearrange("p (a b) n -> p a b n", a=2),
                                             z_ps[:, g % 2, :, 0:2 * (N + 1)].rearrange("p a (b n) -> p a b n", b=2)[:, :, :, 0:N],
                                             ACT.Copy).then_inc(z_hi_ready, 1)

            run(act, body)
            with act.Fori(0, B // SLOTS) as j:
                for s in range(SLOTS):
                    act.wait_ge(y_ready, SLOTS * j + s + 1)
                    act.dma_start(y[bass.ds(SLOTS * j + s, 1)].rearrange("g n f -> n (g f)"), x1_in[:, s]).then_inc(y_stored[s], 16)

        @block.vector
        def _(dve):
            for e in range(E):
                dve.wait_ge(ew_hi_ready, e + 1)
                nc.vector.tensor_tensor(ew_lo[:, e], ew_raw[:, e % 2], ew_hi[:, e], ALU.subtract).then_inc(ew_split, 1)
            dve.wait_ge(consts, 1)
            dve.wait_ge(const_loaded, 64)

            def body(i, mix, expert):
                for token, g in tokens(DVE_ORDER, mix, expert):
                    if token == "N":
                        wait(dve, x1_loaded, 16 * (i + 1))
                        for k in range(G):
                            last = nc.vector.bn_stats(bn[:, k], x1_in[:, k])
                        last.then_inc(bn_done, 1)
                        wait(dve, bn_done, i + 1)
                        halves_combined(nc, bn, mean_sum, mean_diff, m2).then_inc(halves_done, 1)
                        wait(dve, halves_done, i + 1)
                        wait(dve, shift_ready, i)
                        scaled_moments(nc, D, mean_sum, mean_diff, m2, neg_mean).then_inc(scaled_done, 1)
                        wait(dve, scaled_done, i + 1)
                        nc.vector.scalar_tensor_tensor(out=var_eps[:], in0=mean_diff[:], scalar=0.25, in1=m2[:],
                                                       op0=ALU.mult, op1=ALU.add).then_inc(var_ready, 1)
                    elif token == "J":
                        wait(dve, adj_transposed, i + 1)
                        wait(dve, z_made, G * i)
                        nc.vector.tensor_copy(adjT[:, :, 0:N], adjT_ps[:]).then_inc(adjT_ready, 1)
                    elif token == "Z":
                        n = G * i + g
                        wait(dve, z_hi_ready, n + 1)
                        wait(dve, router_scored, i)
                        z = z_ps[:, g % 2, :, 0:2 * (N + 1)].rearrange("p a (b n) -> p a b n", b=2)
                        nc.vector.tensor_copy(mean_h[:, g].rearrange("p (a b) -> p a b", a=2), z[:, :, :, N]).then_inc(mean_ready, 1)
                        nc.vector.tensor_tensor(z_lo[:, g].rearrange("p (a b) n -> p a b n", a=2), z[:, :, :, 0:N],
                                                z_hi[:, g].rearrange("p (a b) n -> p a b n", a=2),
                                                ALU.subtract).then_inc(z_split, 1)
                    elif token == "M":
                        wait(dve, router_scored, i + 1)
                        nc.vector.tensor_tensor(score[:], router_ps[0:1, 0:G * E].rearrange("p (g e) -> p g e", g=G),
                                                rb[:].unsqueeze(1).to_broadcast([1, G, E]), ALU.add).then_inc(router_step, 1)
                        wait(dve, router_step, 4 * i + 1)
                        nc.vector.tensor_reduce(score_max[:], score[:], X, ALU.max).then_inc(router_step, 1)
                        wait(dve, router_step, 4 * i + 2)
                        nc.vector.tensor_tensor(best[:], score[:], score_max[:].unsqueeze(2).to_broadcast([1, G, E]),
                                                ALU.is_ge).then_inc(router_step, 1)
                        wait(dve, router_step, 4 * i + 3)
                        nc.vector.tensor_tensor(candidate[:], best[:], expert_less_e[:].unsqueeze(1).to_broadcast([1, G, E]),
                                                ALU.mult).then_inc(router_step, 1)
                        wait(dve, router_step, 4 * i + 4)
                        nc.vector.tensor_reduce(first[:], candidate[:], X, ALU.min).then_inc(first_ready, 1)
                        wait(dve, first_ready, i + 1)
                        nc.vector.tensor_scalar(top1[:, bass.ds(G * i, G)], first[:], float(E), float(E - 1), ALU.add,
                                                ALU.min).then_inc(routed, 1)

            run(dve, body)

            steps = 0

            def then_wait(instruction):
                nonlocal steps
                steps += 1
                instruction.then_inc(moment_step, 1)
                dve.wait_ge(moment_step, steps)

            dve.wait_ge(routed, GROUPS)
            for e in range(E):
                nc.vector.tensor_scalar(is_expert[:, e], top1[:], float(e), None, ALU.is_equal).then_inc(counted, 1)
            dve.wait_ge(counted, E)
            then_wait(nc.vector.tensor_reduce(count[:], is_expert[:], X, ALU.add))
            then_wait(nc.vector.tensor_scalar(count[:], count[:], float(N), 1.0, ALU.mult, ALU.max))
            nc.vector.reciprocal(inv_count1[:], count[:]).then_inc(count_ready, 1)
            dve.wait_ge(moments_made, 1)
            MOMENTS = 2 * E * KC
            then_wait(nc.vector.tensor_copy(inv_count[:], router_ps[:, MOMENTS:MOMENTS + E]))
            for t in range(2):
                last = nc.vector.tensor_tensor(
                    moment[:, t], router_ps[:, t * E * KC:(t + 1) * E * KC].rearrange("p (e c) -> p e c", e=E),
                    inv_count[:].unsqueeze(2).to_broadcast([128, E, KC]), ALU.mult)
            then_wait(last)
            then_wait(nc.vector.tensor_tensor(mean_sq[:], moment[:, 0], moment[:, 0], ALU.mult))
            then_wait(nc.vector.tensor_tensor(var[:], moment[:, 1], mean_sq[:], ALU.subtract))
            nc.vector.tensor_scalar(var[:], var[:], EPS, None, ALU.add).then_inc(var_all_ready, 1)
            dve.wait_ge(inv_std_ready, 1)
            then_wait(nc.vector.tensor_tensor(coef[:, 0], inv_std[:], gamma_sb[:], ALU.mult))
            then_wait(nc.vector.tensor_tensor(mean_sq[:], moment[:, 0], coef[:, 0], ALU.mult))
            nc.vector.tensor_tensor(coef[:, 1], beta_sb[:], mean_sq[:], ALU.subtract).then_inc(coef_ready, 1)
            for n in range(2 * E):
                dve.wait_ge(rows_made, n + 1)
                nc.vector.tensor_copy(coef_rows[:, n // E, n % E], out_ps[:, n % 2]).then_inc(rows_ready, 1)
            dve.wait_ge(rows_ready, 2 * E)

            LAG = 2

            def finish(n, s):
                dve.wait_ge(shifted, n + 1)
                nc.vector.scalar_tensor_tensor(out=x1_in[:, s], in0=out_sb[:, s], scalar=0.0, in1=x1_in[:, s],
                                               op0=ALU.max, op1=ALU.add).then_inc(y_ready, 1)

            with dve.Fori(0, B // SLOTS) as j:
                for s in range(SLOTS + LAG):
                    if s < SLOTS:
                        n = SLOTS * j + s
                        e = dve.value_load(top1[0:1, bass.ds(n, 1)], min_val=0, max_val=E - 1)
                        dve.wait_ge(slot_loaded[s], 32 * (j + 1))
                        nc.vector.tensor_tensor(out_sb[:, s], out_sb[:, s],
                                                coef_rows[:, 0, bass.ds(e, 1)].rearrange("p a f -> p (a f)"),
                                                ALU.mult).then_inc(scaled, 1)
                    if s >= LAG:
                        finish(SLOTS * j + s - LAG, s - LAG)

        @block.tensor
        def _(pe):
            pe.wait_ge(consts, 1)
            pe.wait_ge(const_loaded, 64)
            pe.wait_ge(ew_split, E)

            def body(i, mix, expert):
                for token, g in tokens(PE_ORDER, mix, expert):
                    if token == "J":
                        wait(pe, adj2_loaded, 16 * (i + 1))
                        wait(pe, adjT_ready, i)
                        for k in range(G):
                            last = nc.tensor.transpose(adjT_ps[:, k], adj_in2[:, k], ident[:])
                        last.then_inc(adj_transposed, 1)
                    elif token == "Z":
                        n = G * i + g
                        wait(pe, h2_ready, n + 1)
                        wait(pe, adjT_ready, i + 1)
                        wait(pe, z_split, n - 1)
                        for c in range(KC):
                            at = (c % 2) * (N + 1)
                            last = nc.tensor.matmul(z_ps[:, g % 2, c // 2, at:at + N + 1], h2[:, g, 128 * c:128 * c + 128],
                                                    adjT[:, g], start=True, stop=True)
                        last.then_inc(z_made, 1)
                    elif token == "M":
                        wait(pe, mean_ready, G * (i + 1))
                        wait(pe, routed, i)
                        for k in range(G):
                            for c in range(KC):
                                last = nc.tensor.matmul(router_ps[0:1, E * k:E * k + E], mean_h[:, k, c:c + 1], rw[:, c],
                                                        start=(c == 0), stop=(c == KC - 1))
                        last.then_inc(router_scored, 1)
                    elif token == "P":
                        n = G * (i - 1) + g
                        if g == 0:
                            wait(pe, routed, i)
                        e = pe.value_load(top1[0:1, bass.ds(n, 1)], min_val=0, max_val=E - 1)
                        wait(pe, z_split, n + 1)
                        wait(pe, squared, n - 1)

                        def of_expert(w, c):
                            return w[:, bass.ds(e, 1), c].rearrange("p a f -> p (a f)")

                        exact_product(nc, out_ps[:, g % 2], [z_hi[:, g, c] for c in range(KC)], [z_lo[:, g, c] for c in range(KC)],
                                      [of_expert(ew_hi, c) for c in range(KC)], [of_expert(ew_lo, c) for c in range(KC)]
                                      ).then_inc(out_made, 1)

            run(pe, body)

            pe.wait_ge(summed, B)
            pe.wait_ge(count_ready, 1)
            pe.wait_ge(routed, GROUPS)
            for t in range(2):
                for e in range(E):
                    for c in range(KC):
                        at = (t * E + e) * KC + c
                        nc.tensor.matmul(router_ps[:, at:at + 1], sums[:, t, e, 128 * c:128 * c + 128], ones[:, 0:1],
                                         start=True, stop=True)
            MOMENTS = 2 * E * KC
            nc.tensor.matmul(router_ps[:, MOMENTS:MOMENTS + E], ones[0:1, :], inv_count1[:],
                             start=True, stop=True).then_inc(moments_made, 1)
            pe.wait_ge(coef_ready, 1)
            for n in range(2 * E):
                if n >= 2:
                    pe.wait_ge(rows_ready, n - 1)
                for c in range(KC):
                    last = nc.tensor.transpose(out_ps[:, n % 2, 128 * c:128 * c + 128],
                                               coef[:, n // E, n % E, c:c + 1].to_broadcast([128, 128]), ident[:])
                last.then_inc(rows_made, 1)


def program(nc, x, adj, wq, wk, wv, wo, router_w, router_b, expert_w, gamma, beta, y):
    B, N, D = x.shape
    x1_dram = nc.dram_tensor("x1_dram", [B, N, D], F32, kind="Internal").ap()
    out_dram = nc.dram_tensor("out_dram", [B, N, D], F32, kind="Internal").ap()
    with ExitStack() as outer:
        def sem(name):
            return outer.enter_context(nc.semaphore(name))

        ident = outer.enter_context(nc.sbuf_tensor("ident", [128, 128], F32))
        ident_step = sem("ident_step")
        with nc.Block() as block:

            @block.gpsimd
            def _(pool):
                nc.gpsimd.memset(ident[:], 0.0).then_inc(ident_step, 1)
                pool.wait_ge(ident_step, 1)
                nc.gpsimd.affine_select(out=ident[:], in_=ident[:], compare_op=ALU.not_equal, fill=1.0, base=0,
                                        pattern=[[-1, 128]], channel_multiplier=1).then_inc(ident_step, 1)
                pool.wait_ge(ident_step, 2)

        with ExitStack() as ctx:
            attention_layer(nc, ctx, sem, ident, x, adj, (wq, wk, wv, wo), x1_dram)
        with ExitStack() as ctx:
            expert_layer(nc, ctx, sem, ident, x1_dram, adj, router_w, router_b, expert_w, gamma, beta, out_dram, y)


def kernel(x, adj, L0_gnn_Wq, L0_gnn_Wk, L0_gnn_Wv, L0_gnn_Wo, L1_gnn_router_w, L1_gnn_router_b, L1_gnn_expert_w,
           L1_gnn_bn_gamma, L1_gnn_bn_beta):
    import numpy as np
    import concourse.bacc as bacc
    from concourse.bass_utils import run_bass_kernel_spmd

    E, D = np.shape(L1_gnn_bn_gamma)
    C = D // 128

    def by_feature(a):
        return np.asarray(a).reshape(E, C, 128).transpose(2, 0, 1)

    inputs = {
        "x": x,
        "adj": adj,
        "wq": np.asarray(L0_gnn_Wq).T,
        "wk": np.asarray(L0_gnn_Wk).T,
        "wv": np.asarray(L0_gnn_Wv).T,
        "wo": np.asarray(L0_gnn_Wo).T,
        "router_w": np.asarray(L1_gnn_router_w).reshape(C, 128, E).transpose(1, 0, 2),
        "router_b": np.asarray(L1_gnn_router_b).reshape(1, E),
        "expert_w": L1_gnn_expert_w,
        "gamma": by_feature(L1_gnn_bn_gamma),
        "beta": by_feature(L1_gnn_bn_beta),
    }
    arrays = {f"in_{name}": np.ascontiguousarray(a) for name, a in inputs.items()}
    nc = bacc.Bacc("TRN2", target_bir_lowering=False, num_devices=1)
    args = [nc.dram_tensor(name, a.shape, mybir.dt.from_np(a.dtype), kind="ExternalInput").ap() for name, a in arrays.items()]
    y = nc.dram_tensor("y", np.shape(x), F32, kind="ExternalOutput").ap()
    program(nc, *args, y)
    return run_bass_kernel_spmd(nc, [arrays], core_ids=[0]).results[0]["y"]
```

```python
from contextlib import ExitStack

import concourse.bass as bass
from concourse import mybir

F32 = mybir.dt.float32
F32R = mybir.dt.float32r
I32 = mybir.dt.int32
ALU = mybir.AluOpType
ACT = mybir.ActivationFunctionType
X = mybir.AxisListType.X

HEADS = 16
EPS = 1e-5


def wait(engine, semaphore, value):
    if not isinstance(value, int) or value > 0:
        engine.wait_ge(semaphore, value)


def exact_product(nc, out, a_hi, a_lo, b_hi, b_lo):
    terms = [t for k in range(len(a_hi)) for t in ((a_hi[k], b_hi[k]), (a_hi[k], b_lo[k]), (a_lo[k], b_hi[k]))]
    for n, (a, b) in enumerate(terms):
        last = nc.tensor.matmul(out, a, b, start=(n == 0), stop=(n == len(terms) - 1))
    return last


def halves_combined(nc, bn, mean_sum, mean_diff, m2):
    nc.vector.tensor_tensor(mean_sum[:], bn[:, :, 1], bn[:, :, 4], ALU.add)
    nc.vector.tensor_tensor(mean_diff[:], bn[:, :, 1], bn[:, :, 4], ALU.subtract)
    return nc.vector.tensor_tensor(m2[:], bn[:, :, 2], bn[:, :, 5], ALU.add)


def scaled_moments(nc, count, mean_sum, mean_diff, m2, neg_mean):
    nc.vector.tensor_scalar(neg_mean[:], mean_sum[:], -0.5, None, ALU.mult)
    nc.vector.tensor_tensor(mean_diff[:], mean_diff[:], mean_diff[:], ALU.mult)
    return nc.vector.tensor_scalar(m2[:], m2[:], 1.0 / count, EPS, ALU.mult, ALU.add)


def attention_layer(nc, ctx, sem, ident, x, adj, weights, x1_dram):
    B, N, D = x.shape
    PAIRS = B // 2
    KC = D // 128
    R = 4
    C = HEADS // R
    HD = D // HEADS
    STEPS = 2 * C
    SCALE = float(D) ** -0.5
    STACKS = 16 * 3 * R

    def sb(name, shape, dt=F32):
        return ctx.enter_context(nc.sbuf_tensor(name, shape, dt))

    def ps(name, shape):
        return ctx.enter_context(nc.psum_tensor(name, shape, F32))

    w_hi = sb("w_hi", [N, 4, KC, D], F32R)
    w_lo = sb("w_lo", [N, 4, KC, D], F32R)
    x_in = sb("x_in", [N, 2, D])
    h = sb("h", [N, 2, D])
    hT_hi = sb("hT_hi", [128, KC, 2, N], F32R)
    hT_lo = sb("hT_lo", [128, KC, 2, N], F32R)
    Q_LO, Q_HI, K_HI, K_LO = range(4)
    qk = sb("qk", [128, 4, 2, C, N], F32R)
    stack = sb("stack", [3 * HD, 2, R, 2, C, N], F32R)
    v = sb("v", [N, 2, D])
    logits = sb("logits", [N, 4, R, N])
    prob = sb("prob", [N, 4, R, N])
    probT = sb("probT", [N, 4, R, N])
    o_hi = sb("o_hi", [128, C, N], F32R)
    o_lo = sb("o_lo", [128, C, N], F32R)
    x_res = sb("x_res", [N, 2, D])
    adj_in = sb("adj_in", [N, 2, N])
    adj2 = sb("adj2", [N, 2, N])
    bn = sb("bn", [N, 2, 6])
    mean_sum = sb("mean_sum", [N, 2])
    mean_diff = sb("mean_diff", [N, 2])
    m2 = sb("m2", [N, 2])
    var_eps = sb("var_eps", [N, 2])
    neg_mean = sb("neg_mean", [N, 2])
    minus_half = sb("minus_half", [N, 2])
    rstd = sb("rstd", [N, 2])
    shift = sb("shift", [N, 2])
    neg_max = sb("neg_max", [N, 4, R])
    abs_max = sb("abs_max", [N, 4, R])
    row_sum = sb("row_sum", [N, 4, R])
    inv_sum = sb("inv_sum", [N, 4, R])
    norm = sb("norm", [N, 4, R])

    scores_ps = ps("scores_ps", [N, 2, R, N])
    probT_ps = ps("probT_ps", [N, 2, R, N])
    o_ps = ps("o_ps", [128, C, N])
    bank = ps("bank", [128, 3, 512])

    w_loaded, w_hi_ready, w_split = sem("w_loaded"), sem("w_hi_ready"), sem("w_split")
    x_loaded, var_ready, rstd_ready, shift_ready, h_ready = map(
        sem, ("x_loaded", "var_ready", "rstd_ready", "shift_ready", "h_ready"))
    bn_done, halves_done, scaled_done = sem("bn_done"), sem("halves_done"), sem("scaled_done")
    h_transposed, hT_hi_ready, hT_split = sem("h_transposed"), sem("hT_hi_ready"), sem("hT_split")
    qk_projected, qk_hi_ready, qk_split = sem("qk_projected"), sem("qk_hi_ready"), sem("qk_split")
    stacked = [sem("stacked0"), sem("stacked1")]
    v_projected, v_copied = sem("v_projected"), sem("v_copied")
    adj_loaded, adj_doubled = sem("adj_loaded"), sem("adj_doubled")
    scored, logits_ready, neg_max_ready, abs_max_ready = map(
        sem, ("scored", "logits_ready", "neg_max_ready", "abs_max_ready"))
    exp_done, inverted, norm_ready, normed = map(sem, ("exp_done", "inverted", "norm_ready", "normed"))
    transposed, probT_ready, applied = sem("transposed"), sem("probT_ready"), sem("applied")
    o_hi_ready, o_split, o_projected = sem("o_hi_ready"), sem("o_split"), sem("o_projected")
    x_res_loaded = [sem("x_res_loaded0"), sem("x_res_loaded1")]
    x1_ready = sem("x1_ready")
    x1_stored = [sem("x1_stored0"), sem("x1_stored1")]
    half_ready = sem("half_ready")

    PE_ORDER = """S0 T6' W5' H1' O0'
                  S1 T7' W6' Q0
                  S2 T0 W7' Q1
                  S3 T1 W0 Q2
                  S4 T2 W1 Q3
                  S5 T3 W2 O1'
                  S6 T4 W3 V0
                  S7 T5 W4 H0 V1"""
    ACT_ORDER = """H1' C6' E0
                   C7' E1
                   Q0 C0 O1' E2 V1'
                   Q1 C1 E3
                   Q2 C2 E4
                   Q3 C3 E5 A0
                   C4 O0 E6 A1
                   V0 C5 E7 H0"""
    DVE_ORDER = """R7' L0 H1' B0 N0
                   R0 L1 X0' B1 N1
                   R1 L2 Q0 O1' B2
                   R2 L3 Q1 B3 M
                   R3 L4 Q2 B4
                   R4 L5 Q3 B5
                   R5 L6 O0 X1' B6
                   R6 L7 H0 B7"""
    POOL_ORDER = "P7' D1' P0 P1 P2 P3 G P4 D0 P5 P6"
    SP_ORDER = "X K1' J Z1' Y0' Z0 K0 Y1'"
    AHEAD = {"sp": dict(X=2, J=1, K=1), "pe": dict(Q=1, V=1, H=2), "act": dict(Q=1, V=1, H=2, A=2),
             "dve": dict(Q=1, H=2, N=2, M=2), "pool": dict(G=2, D=1)}
    Q_BANK, V_BANK, O_BANK, H_BANK = (2, 1, 0, 2), (2, 0), (1, 1), (1, 2)

    def tokens(engine, order, i):
        for t in order.split():
            pair = i + (AHEAD[engine].get(t[0], 0) - t.endswith("'"))
            if not isinstance(pair, int) or 0 <= pair < PAIRS:
                yield t[0], int(t[1:].strip("'") or 0), pair

    def exists(pair):
        return not isinstance(pair, int) or pair < PAIRS

    def run(engine, body):
        for i in (-2, -1, 0, 1):
            body(i)
        with engine.Fori(2, PAIRS - 2) as i:
            body(i)
        for i in (PAIRS - 2, PAIRS - 1, PAIRS):
            body(i)

    with nc.Block() as block:

        @block.sync
        def _(sp):
            for n, w in enumerate(weights):
                raw = (logits, prob, probT)[n % 3]
                if n >= 3:
                    sp.wait_ge(w_split, n - 2)
                sp.dma_start(raw[:].rearrange("p k r n -> p k (r n)"),
                             w.rearrange("(k p) f -> p k f", p=128)).then_inc(w_loaded, 16)
                if n == 0:
                    sp.dma_start(x_in[:], x[0:2].rearrange("g n f -> n g f")).then_inc(x_loaded, 16)
                sp.wait_ge(w_loaded, 16 * (n + 1))

            def body(i):
                for token, g, j in tokens("sp", SP_ORDER, i):
                    if token == "X" and not (isinstance(j, int) and j == 0):
                        wait(sp, h_ready, 2 * j)
                        sp.dma_start(x_in[:], x[bass.ds(2 * j, 2)].rearrange("g n f -> n g f")).then_inc(x_loaded, 16)
                    elif token == "J":
                        wait(sp, adj_doubled, 2 * j)
                        sp.dma_start(adj_in[:], adj[bass.ds(2 * j, 2)].rearrange("g n m -> n g m")).then_inc(adj_loaded, 16)
                    elif token == "Z":
                        wait(sp, x1_stored[g], 16 * j)
                        sp.dma_start(x_res[:, g, :], x[bass.ds(2 * j + g, 1)].rearrange("g n f -> n (g f)")).then_inc(x_res_loaded[g], 16)
                    elif token == "Y":
                        wait(sp, x1_ready, 2 * j + g + 1)
                        sp.dma_start(x1_dram[bass.ds(2 * j + g, 1)].rearrange("g n f -> n (g f)"), x_res[:, g, :]).then_inc(x1_stored[g], 16)
                    elif token == "K":
                        wait(sp, qk_split, 4 * (j + 1))
                        wait(sp, scored, STEPS * (j - 1) + C * (g + 1))
                        for s, (a, b) in enumerate(((Q_HI, K_HI), (Q_LO, K_HI), (Q_HI, K_LO))):
                            for r in range(R):
                                sp.dma_start(
                                    stack[HD * s:HD * s + HD, g, r].bitcast(F32).rearrange("p t c n -> p t (c n)"),
                                    qk[HD * r:HD * r + HD, a:b + 1:b - a, g].bitcast(F32).rearrange("p t c n -> p t (c n)"),
                                ).then_inc(stacked[g], 16)

            run(sp, body)
            for g in range(2):
                sp.wait_ge(x1_stored[g], 16 * PAIRS)

        @block.gpsimd
        def _(pool):
            nc.gpsimd.memset(minus_half[:], -0.5).then_inc(half_ready, 1)
            pool.wait_ge(half_ready, 1)

            def body(i):
                for token, k, j in tokens("pool", POOL_ORDER, i):
                    if token == "P":
                        slot = k % 4
                        wait(pool, norm_ready, STEPS * j + k + 1)
                        nc.gpsimd.tensor_tensor(prob[:, slot], prob[:, slot],
                                                norm[:, slot].unsqueeze(2).to_broadcast([N, R, N]),
                                                ALU.mult).then_inc(normed, 1)
                    elif token == "G":
                        wait(pool, var_ready, j + 1)
                        wait(pool, h_ready, 2 * j)
                        nc.gpsimd.tensor_tensor(rstd[:], var_eps[:], minus_half[:], ALU.pow).then_inc(rstd_ready, 1)
                        wait(pool, rstd_ready, j + 1)
                        nc.gpsimd.tensor_tensor(shift[:], neg_mean[:], rstd[:], ALU.mult).then_inc(shift_ready, 1)
                    elif token == "D":
                        wait(pool, adj_loaded, 16 * (j + 1))
                        wait(pool, logits_ready, STEPS * (j - 1) + C * (k + 1))
                        nc.gpsimd.tensor_tensor(adj2[:, k], adj_in[:, k], adj_in[:, k], ALU.add).then_inc(adj_doubled, 1)

            run(pool, body)

        @block.scalar
        def _(act):
            for n in range(4):
                act.wait_ge(w_loaded, 16 * (n + 1))
                raw = (logits, prob, probT)[n % 3]
                nc.scalar.activation(w_hi[:, n], raw[:].rearrange("p k r n -> p k (r n)"), ACT.Copy).then_inc(w_hi_ready, 1)

            def body(i):
                for token, k, j in tokens("act", ACT_ORDER, i):
                    slot = k % 4
                    if token == "E":
                        wait(act, neg_max_ready, STEPS * j + k + 1)
                        wait(act, transposed, STEPS * j + k - 3)
                        for r in range(R):
                            last = nc.scalar.activation(prob[:, slot, r], logits[:, slot, r], ACT.Exp,
                                                        bias=neg_max[:, slot, r:r + 1],
                                                        accum_out=row_sum[:, slot, r:r + 1])
                        last.then_inc(exp_done, 1)
                    elif token == "C":
                        wait(act, transposed, STEPS * j + k + 1)
                        wait(act, applied, STEPS * j + k - 3)
                        nc.scalar.activation(probT[:, slot], probT_ps[:, k % 2], ACT.Copy).then_inc(probT_ready, 1)
                    elif token == "O":
                        wait(act, applied, STEPS * j + C * (k + 1))
                        wait(act, o_projected, 2 * j + k)
                        nc.scalar.activation(o_hi[:], o_ps[:], ACT.Copy).then_inc(o_hi_ready, 1)
                    elif token == "Q":
                        wait(act, qk_projected, 4 * j + k + 1)
                        if k == 0:
                            for g in range(2):
                                wait(act, stacked[g], STACKS * j)
                        t, c = (Q_HI, K_HI)[k // 2], 2 * (k % 2)
                        nc.scalar.activation(qk[:, t, :, c:c + 2].rearrange("p g c n -> p c g n"),
                                             bank[:, Q_BANK[k]].rearrange("p (c g n) -> p c g n", c=2, g=2),
                                             ACT.Copy).then_inc(qk_hi_ready, 1)
                    elif token == "V":
                        wait(act, v_projected, 2 * j + k + 1)
                        wait(act, applied, STEPS * (j - 1) + C * (k + 1))
                        nc.scalar.activation(v[:, k], bank[:, V_BANK[k]], ACT.Copy).then_inc(v_copied, 1)
                    elif token == "A":
                        wait(act, shift_ready, j + 1)
                        wait(act, h_transposed, 2 * (j - 1) + k + 1)
                        nc.scalar.activation(h[:, k], x_in[:, k], ACT.Relu, bias=shift[:, k:k + 1],
                                             scale=rstd[:, k:k + 1]).then_inc(h_ready, 1)
                    elif token == "H":
                        wait(act, h_transposed, 2 * j + k + 1)
                        nc.scalar.activation(hT_hi[:, :, k], bank[:, H_BANK[k]].rearrange("p (c n) -> p c n", n=N),
                                             ACT.Copy).then_inc(hT_hi_ready, 1)

            run(act, body)

        @block.vector
        def _(dve):
            for n in range(4):
                dve.wait_ge(w_hi_ready, n + 1)
                raw = (logits, prob, probT)[n % 3]
                nc.vector.tensor_tensor(w_lo[:, n], raw[:].rearrange("p k r n -> p k (r n)"), w_hi[:, n],
                                        ALU.subtract).then_inc(w_split, 1)

            def body(i):
                for token, k, j in tokens("dve", DVE_ORDER, i):
                    slot = k % 4
                    if token == "L":
                        wait(dve, scored, STEPS * j + k + 1)
                        wait(dve, exp_done, STEPS * j + k - 3)
                        if k % C == 0:
                            wait(dve, adj_doubled, 2 * j + k // C + 1)
                            if isinstance(j, int) and j == 0:
                                dve.wait_ge(w_split, 4)
                        nc.vector.scalar_tensor_tensor(
                            out=logits[:, slot], in0=scores_ps[:, k % 2], scalar=SCALE,
                            in1=adj2[:, k // C].unsqueeze(1).to_broadcast([N, R, N]),
                            op0=ALU.mult, op1=ALU.add).then_inc(logits_ready, 1)
                        wait(dve, logits_ready, STEPS * j + k + 1)
                        nc.vector.tensor_reduce(neg_max[:, slot], logits[:, slot], X, ALU.max,
                                                negate=True).then_inc(neg_max_ready, 1)
                    elif token == "B":
                        nc.vector.tensor_reduce(abs_max[:, slot], logits[:, slot], X, ALU.max,
                                                apply_absolute_value=True).then_inc(abs_max_ready, 1)
                    elif token == "R":
                        wait(dve, exp_done, STEPS * j + k + 1)
                        wait(dve, abs_max_ready, STEPS * j + k + 1)
                        nc.vector.reciprocal(inv_sum[:, slot], row_sum[:, slot]).then_inc(inverted, 1)
                        wait(dve, inverted, STEPS * j + k + 1)
                        wait(dve, normed, STEPS * j + k - 3)
                        nc.vector.scalar_tensor_tensor(
                            out=norm[:, slot], in0=abs_max[:, slot], scalar=0.0, in1=inv_sum[:, slot],
                            op0=ALU.not_equal, op1=ALU.mult).then_inc(norm_ready, 1)
                    elif token == "O":
                        wait(dve, o_hi_ready, 2 * j + k + 1)
                        nc.vector.tensor_tensor(o_lo[:], o_ps[:], o_hi[:], ALU.subtract).then_inc(o_split, 1)
                    elif token == "X":
                        wait(dve, o_projected, 2 * j + k + 1)
                        wait(dve, x_res_loaded[k], 16 * (j + 1))
                        nc.vector.tensor_tensor(x_res[:, k], bank[:, O_BANK[k]], x_res[:, k],
                                                ALU.add).then_inc(x1_ready, 1)
                    elif token == "Q":
                        wait(dve, qk_hi_ready, 4 * j + k + 1)
                        hi, lo = ((Q_HI, Q_LO), (K_HI, K_LO))[k // 2]
                        c = 2 * (k % 2)
                        nc.vector.tensor_tensor(qk[:, lo, :, c:c + 2].rearrange("p g c n -> p c g n"),
                                                bank[:, Q_BANK[k]].rearrange("p (c g n) -> p c g n", c=2, g=2),
                                                qk[:, hi, :, c:c + 2].rearrange("p g c n -> p c g n"),
                                                ALU.subtract).then_inc(qk_split, 1)
                    elif token == "N":
                        wait(dve, x_loaded, 16 * (j + 1))
                        nc.vector.bn_stats(bn[:, k], x_in[:, k]).then_inc(bn_done, 1)
                    elif token == "M":
                        wait(dve, bn_done, 2 * (j + 1))
                        halves_combined(nc, bn, mean_sum, mean_diff, m2).then_inc(halves_done, 1)
                        wait(dve, halves_done, j + 1)
                        wait(dve, shift_ready, j)
                        scaled_moments(nc, D, mean_sum, mean_diff, m2, neg_mean).then_inc(scaled_done, 1)
                        wait(dve, scaled_done, j + 1)
                        nc.vector.scalar_tensor_tensor(out=var_eps[:], in0=mean_diff[:], scalar=0.25, in1=m2[:],
                                                       op0=ALU.mult, op1=ALU.add).then_inc(var_ready, 1)
                    elif token == "H":
                        wait(dve, hT_hi_ready, 2 * j + k + 1)
                        nc.vector.tensor_tensor(hT_lo[:, :, k], bank[:, H_BANK[k]].rearrange("p (c n) -> p c n", n=N),
                                                hT_hi[:, :, k], ALU.subtract).then_inc(hT_split, 1)

            run(dve, body)

        @block.tensor
        def _(pe):
            def body(i):
                for token, k, j in tokens("pe", PE_ORDER, i):
                    g, c, slot = k // C, k % C, k % 4
                    if token == "S":
                        if c == 0:
                            wait(pe, stacked[g], STACKS * (j + 1))
                        wait(pe, logits_ready, STEPS * j + k - 1)
                        for r in range(R):
                            last = nc.tensor.matmul(scores_ps[:, k % 2, r], stack[:, g, r, 0, c], stack[:, g, r, 1, c],
                                                    start=True, stop=True)
                        last.then_inc(scored, 1)
                    elif token == "T":
                        wait(pe, normed, STEPS * j + k + 1)
                        wait(pe, probT_ready, STEPS * j + k - 1)
                        for r in range(R):
                            last = nc.tensor.transpose(probT_ps[:, k % 2, r], prob[:, slot, r], ident[:])
                        last.then_inc(transposed, 1)
                    elif token == "W":
                        wait(pe, probT_ready, STEPS * j + k + 1)
                        if c == 0:
                            wait(pe, v_copied, 2 * j + g + 1)
                            wait(pe, o_split, 2 * j + g)
                        for r in range(R):
                            f = HD * (R * c + r)
                            last = nc.tensor.matmul(o_ps[HD * r:HD * r + HD, c], v[:, g, f:f + HD], probT[:, slot, r],
                                                    start=True, stop=True)
                        last.then_inc(applied, 1)
                    elif token == "O":
                        wait(pe, o_split, 2 * j + k + 1)
                        if exists(j + 2):
                            wait(pe, *((hT_split, 2 * (j + 2) + 1), (qk_split, 4 * (j + 2) + 2))[k])
                        else:
                            wait(pe, x1_ready, 2 * j + k)
                        exact_product(nc, bank[:, O_BANK[k]], [o_hi[:, c] for c in range(C)], [o_lo[:, c] for c in range(C)],
                                      [w_hi[:, 3, c] for c in range(C)], [w_lo[:, 3, c] for c in range(C)]
                                      ).then_inc(o_projected, 1)
                    elif token == "Q":
                        if isinstance(j, int) and j == 0 and k % 2 == 0:
                            pe.wait_ge(w_split, k // 2 + 1)
                        wait(pe, *((hT_split, 2 * (j + 1)), (x1_ready, 2 * (j - 2) + 1), (v_copied, 2 * j),
                                   (qk_split, 4 * j + 1))[k])
                        for half in range(2):
                            m = 128 * (2 * (k % 2) + half)
                            last = exact_product(nc, bank[:, Q_BANK[k], 256 * half:256 * half + 256],
                                                 [w_hi[:, k // 2, kc, m:m + 128] for kc in range(KC)],
                                                 [w_lo[:, k // 2, kc, m:m + 128] for kc in range(KC)],
                                                 [hT_hi[:, kc] for kc in range(KC)], [hT_lo[:, kc] for kc in range(KC)])
                        last.then_inc(qk_projected, 1)
                    elif token == "V":
                        if isinstance(j, int) and j == 0 and k == 0:
                            pe.wait_ge(w_split, 3)
                        wait(pe, qk_split, 4 * j + (4, 3)[k])
                        exact_product(nc, bank[:, V_BANK[k]], [hT_hi[:, kc, k] for kc in range(KC)],
                                      [hT_lo[:, kc, k] for kc in range(KC)],
                                      [w_hi[:, 2, kc] for kc in range(KC)], [w_lo[:, 2, kc] for kc in range(KC)]
                                      ).then_inc(v_projected, 1)
                    elif token == "H":
                        wait(pe, h_ready, 2 * j + k + 1)
                        wait(pe, *((x1_ready, 2 * (j - 2)), (v_copied, 2 * (j - 1) + 1))[k])
                        for kc in range(KC):
                            last = nc.tensor.transpose(bank[:, H_BANK[k], 128 * kc:128 * kc + 128],
                                                       h[:, k, 128 * kc:128 * kc + 128], ident[:])
                        last.then_inc(h_transposed, 1)

            run(pe, body)


def expert_layer(nc, ctx, sem, ident, x1_dram, adj, router_w, router_b, expert_w, gamma, beta, out_dram, y):
    B, N, D = x1_dram.shape
    E = expert_w.shape[0]
    KC = D // 128
    G = 4
    GROUPS = B // G
    SLOTS = 2 * G

    def sb(name, shape, dt=F32):
        return ctx.enter_context(nc.sbuf_tensor(name, shape, dt))

    def ps(name, shape):
        return ctx.enter_context(nc.psum_tensor(name, shape, F32))

    ew_raw = sb("ew_raw", [128, 2, KC, D])
    ew_hi = sb("ew_hi", [128, E, KC, D], F32R)
    ew_lo = sb("ew_lo", [128, E, KC, D], F32R)
    x1_in = sb("x1_in", [N, SLOTS, D])
    h2 = x1_in[:, G:]
    out_sb = sb("out_sb", [N, SLOTS, D])
    square = out_sb[:, G:]
    adj_in2 = sb("adj_in2", [N, G, N])
    adjT = sb("adjT", [N, G, N + 1])
    z_hi = sb("z_hi", [128, G, KC, N], F32R)
    z_lo = sb("z_lo", [128, G, KC, N], F32R)
    mean_h = sb("mean_h", [128, G, KC])
    sums = sb("sums", [N, 2, E, D])
    rw = sb("rw", [128, KC, E])
    rb = sb("rb", [1, E])
    expert_less_e = sb("expert_less_e", [1, E])
    score = sb("score", [1, G, E])
    score_max = sb("score_max", [1, G])
    best = sb("best", [1, G, E])
    candidate = sb("candidate", [1, G, E])
    first = sb("first", [1, G])
    top1 = sb("top1", [1, B], I32)
    bn = sb("bn2", [N, G, 6])
    mean_sum = sb("mean_sum2", [N, G])
    mean_diff = sb("mean_diff2", [N, G])
    m2 = sb("m22", [N, G])
    var_eps = sb("var_eps2", [N, G])
    neg_mean = sb("neg_mean2", [N, G])
    minus_half = sb("minus_half2", [N, E * KC])
    rstd = sb("rstd2", [N, G])
    shift = sb("shift2", [N, G])
    ones = sb("ones", [N, 128])
    gamma_sb = sb("gamma_sb", [128, E, KC])
    beta_sb = sb("beta_sb", [128, E, KC])
    is_expert = sb("is_expert", [1, E, B])
    count = sb("count", [1, E])
    inv_count1 = sb("inv_count1", [1, E])
    inv_count = sb("inv_count", [128, E])
    moment = sb("moment", [128, 2, E, KC])
    mean_sq = sb("mean_sq", [128, E, KC])
    var = sb("var", [128, E, KC])
    inv_std = sb("inv_std", [128, E, KC])
    coef = sb("coef", [128, 2, E, KC])
    coef_rows = sb("coef_rows", [N, 2, E, D])

    adjT_ps = ps("adjT_ps", [N, G, N])
    router_ps = ps("router_ps", [128, 512])
    z_ps = ps("z_ps", [128, 2, 2, 512])
    out_ps = ps("out_ps", [N, 2, D])

    const_loaded, ew_loaded, ew_hi_ready, ew_split = map(sem, ("const_loaded", "ew_loaded", "ew_hi_ready", "ew_split"))
    consts = sem("consts")
    x1_loaded, adj2_loaded = sem("x1_loaded"), sem("adj2_loaded")
    bn_done, halves_done, scaled_done, var_ready, rstd_ready, shift_ready, h2_ready = map(
        sem, ("bn_done2", "halves_done2", "scaled_done2", "var_ready2", "rstd_ready2", "shift_ready2", "h2_ready"))
    adj_transposed, adjT_ready = sem("adj_transposed"), sem("adjT_ready")
    z_made, z_hi_ready, mean_ready, z_split = map(sem, ("z_made", "z_hi_ready", "mean_ready", "z_split"))
    router_scored, router_step, first_ready, routed = map(sem, ("router_scored", "router_step", "first_ready", "routed"))
    out_made, out_copied, squared, summed = map(sem, ("out_made", "out_copied", "squared", "summed"))
    out_stored = [sem(f"out_stored{g}") for g in range(G)]
    counted, count_ready, moments_made, moment_step = map(sem, ("counted", "count_ready", "moments_made", "moment_step"))
    var_all_ready, inv_std_ready, coef_ready, rows_made, rows_ready = map(
        sem, ("var_all_ready", "inv_std_ready", "coef_ready", "rows_made", "rows_ready"))
    slot_loaded = [sem(f"slot_loaded{s}") for s in range(SLOTS)]
    y_stored = [sem(f"y_stored{s}") for s in range(SLOTS)]
    scaled, shifted, y_ready = sem("scaled"), sem("shifted"), sem("y_ready")

    PE_ORDER = "P0 J P1 Z0 P2 Z1 P3 Z2 Z3 M"
    ACT_ORDER = "A0 A1 P0 A2 A3 P1 Z0 P2 Z1 P3 Z2 Z3"
    DVE_ORDER = "N J Z0 Z1 Z2 Z3 M"

    def tokens(order, mix, expert):
        on = {**dict.fromkeys("JZMAN", mix), "P": expert}
        return [(t[0], int(t[1:] or 0)) for t in order.split() if on[t[0]]]

    def run(engine, body):
        body(0, True, False)
        body(1, True, True)
        with engine.Fori(2, GROUPS) as i:
            body(i, True, True)
        body(GROUPS, False, True)

    with nc.Block() as block:

        @block.sync
        def _(sp):
            sp.dma_start(rw[:], router_w).then_inc(const_loaded, 16)
            sp.dma_start(rb[:], router_b).then_inc(const_loaded, 16)
            sp.dma_start(gamma_sb[:], gamma).then_inc(const_loaded, 16)
            sp.dma_start(beta_sb[:], beta).then_inc(const_loaded, 16)

            def load(i):
                wait(sp, h2_ready, G * i)
                sp.dma_start(x1_in[:, 0:G], x1_dram[bass.ds(G * i, G)].rearrange("g n f -> n g f")).then_inc(x1_loaded, 16)
                wait(sp, adj_transposed, i)
                sp.dma_start(adj_in2[:], adj[bass.ds(G * i, G)].rearrange("g n m -> n g m")).then_inc(adj2_loaded, 16)

            load(0)
            for e in range(E):
                if e >= 2:
                    sp.wait_ge(ew_split, e - 1)
                if e:
                    sp.wait_ge(ew_loaded, 16 * e)
                sp.dma_start(ew_raw[:, e % 2], expert_w[e].rearrange("(k p) f -> p k f", p=128)).then_inc(ew_loaded, 16)

            def body(i, mix, expert):
                if mix and not (isinstance(i, int) and i == 0):
                    load(i)
                if expert:
                    for g in range(G):
                        wait(sp, out_copied, G * (i - 1) + g + 1)
                        sp.dma_start(out_dram[bass.ds(G * (i - 1) + g, 1)].rearrange("g n f -> n (g f)"), out_sb[:, g]).then_inc(out_stored[g], 16)

            run(sp, body)
            for g in range(G):
                sp.wait_ge(out_stored[g], 16 * GROUPS)
            sp.wait_ge(summed, B)

            def load_slots(j):
                for s in range(SLOTS):
                    wait(sp, y_stored[s], 16 * j)
                    for src, dst in ((out_dram, out_sb), (x1_dram, x1_in)):
                        sp.dma_start(dst[:, s], src[bass.ds(SLOTS * j + s, 1)].rearrange("g n f -> n (g f)")).then_inc(slot_loaded[s], 16)

            load_slots(0)
            with sp.Fori(1, B // SLOTS) as j:
                load_slots(j)
            for s in range(SLOTS):
                sp.wait_ge(y_stored[s], 16 * (B // SLOTS))

        @block.gpsimd
        def _(pool):
            nc.gpsimd.memset(minus_half[:], -0.5)
            nc.gpsimd.memset(ones[:], 1.0)
            nc.gpsimd.memset(sums[:], 0.0)
            for e in range(E):
                nc.gpsimd.memset(expert_less_e[:, e:e + 1], float(e - E))
            nc.gpsimd.memset(adjT[:, :, N:N + 1], 1.0 / N).then_inc(consts, 1)
            pool.wait_ge(consts, 1)

            def body(i, mix, expert):
                if mix:
                    wait(pool, var_ready, i + 1)
                    wait(pool, h2_ready, G * i)
                    nc.gpsimd.tensor_tensor(rstd[:], var_eps[:], minus_half[:, 0:G], ALU.pow).then_inc(rstd_ready, 1)
                    wait(pool, rstd_ready, i + 1)
                    nc.gpsimd.tensor_tensor(shift[:], neg_mean[:], rstd[:], ALU.mult).then_inc(shift_ready, 1)
                if expert:
                    wait(pool, routed, i)
                    for g in range(G):
                        n = G * (i - 1) + g
                        e = pool.value_load(top1[0:1, bass.ds(n, 1)], min_val=0, max_val=E - 1)
                        wait(pool, squared, n + 1)
                        wait(pool, summed, n)
                        for t, src in enumerate((out_sb[:, g], square[:, g])):
                            total = sums[:, t, bass.ds(e, 1)].rearrange("p a f -> p (a f)")
                            last = nc.gpsimd.tensor_tensor(total, total, src, ALU.add)
                        last.then_inc(summed, 1)

            run(pool, body)
            pool.wait_ge(var_all_ready, 1)
            nc.gpsimd.tensor_tensor(inv_std[:].rearrange("p e c -> p (e c)"), var[:].rearrange("p e c -> p (e c)"),
                                    minus_half[:], ALU.pow).then_inc(inv_std_ready, 1)
            pool.wait_ge(rows_ready, 2 * E)
            with pool.Fori(0, B // SLOTS) as j:
                for s in range(SLOTS):
                    n = SLOTS * j + s
                    e = pool.value_load(top1[0:1, bass.ds(n, 1)], min_val=0, max_val=E - 1)
                    pool.wait_ge(scaled, n + 1)
                    nc.gpsimd.tensor_tensor(out_sb[:, s], out_sb[:, s],
                                            coef_rows[:, 1, bass.ds(e, 1)].rearrange("p a f -> p (a f)"),
                                            ALU.add).then_inc(shifted, 1)

        @block.scalar
        def _(act):
            for e in range(E):
                act.wait_ge(ew_loaded, 16 * (e + 1))
                nc.scalar.activation(ew_hi[:, e], ew_raw[:, e % 2], ACT.Copy).then_inc(ew_hi_ready, 1)

            def body(i, mix, expert):
                for token, g in tokens(ACT_ORDER, mix, expert):
                    if token == "A":
                        wait(act, shift_ready, i + 1)
                        wait(act, z_made, G * (i - 1) + g + 1)
                        nc.scalar.activation(h2[:, g], x1_in[:, g], ACT.Relu, bias=shift[:, g:g + 1],
                                             scale=rstd[:, g:g + 1]).then_inc(h2_ready, 1)
                    elif token == "P":
                        n = G * (i - 1) + g
                        wait(act, out_made, n + 1)
                        wait(act, out_stored[g], 16 * (i - 1))
                        wait(act, summed, n - G + 1)
                        nc.scalar.activation(out_sb[:, g], out_ps[:, g % 2], ACT.Copy).then_inc(out_copied, 1)
                        nc.scalar.activation(square[:, g], out_ps[:, g % 2], ACT.Square).then_inc(squared, 1)
                    elif token == "Z":
                        n = G * i + g
                        wait(act, z_made, n + 1)
                        wait(act, out_made, n - G + 1)
                        nc.scalar.activation(z_hi[:, g].rearrange("p (a b) n -> p a b n", a=2),
                                             z_ps[:, g % 2, :, 0:2 * (N + 1)].rearrange("p a (b n) -> p a b n", b=2)[:, :, :, 0:N],
                                             ACT.Copy).then_inc(z_hi_ready, 1)

            run(act, body)
            with act.Fori(0, B // SLOTS) as j:
                for s in range(SLOTS):
                    act.wait_ge(y_ready, SLOTS * j + s + 1)
                    act.dma_start(y[bass.ds(SLOTS * j + s, 1)].rearrange("g n f -> n (g f)"), x1_in[:, s]).then_inc(y_stored[s], 16)

        @block.vector
        def _(dve):
            for e in range(E):
                dve.wait_ge(ew_hi_ready, e + 1)
                nc.vector.tensor_tensor(ew_lo[:, e], ew_raw[:, e % 2], ew_hi[:, e], ALU.subtract).then_inc(ew_split, 1)
            dve.wait_ge(consts, 1)
            dve.wait_ge(const_loaded, 64)

            def body(i, mix, expert):
                for token, g in tokens(DVE_ORDER, mix, expert):
                    if token == "N":
                        wait(dve, x1_loaded, 16 * (i + 1))
                        for k in range(G):
                            last = nc.vector.bn_stats(bn[:, k], x1_in[:, k])
                        last.then_inc(bn_done, 1)
                        wait(dve, bn_done, i + 1)
                        halves_combined(nc, bn, mean_sum, mean_diff, m2).then_inc(halves_done, 1)
                        wait(dve, halves_done, i + 1)
                        wait(dve, shift_ready, i)
                        scaled_moments(nc, D, mean_sum, mean_diff, m2, neg_mean).then_inc(scaled_done, 1)
                        wait(dve, scaled_done, i + 1)
                        nc.vector.scalar_tensor_tensor(out=var_eps[:], in0=mean_diff[:], scalar=0.25, in1=m2[:],
                                                       op0=ALU.mult, op1=ALU.add).then_inc(var_ready, 1)
                    elif token == "J":
                        wait(dve, adj_transposed, i + 1)
                        wait(dve, z_made, G * i)
                        nc.vector.tensor_copy(adjT[:, :, 0:N], adjT_ps[:]).then_inc(adjT_ready, 1)
                    elif token == "Z":
                        n = G * i + g
                        wait(dve, z_hi_ready, n + 1)
                        wait(dve, router_scored, i)
                        z = z_ps[:, g % 2, :, 0:2 * (N + 1)].rearrange("p a (b n) -> p a b n", b=2)
                        nc.vector.tensor_copy(mean_h[:, g].rearrange("p (a b) -> p a b", a=2), z[:, :, :, N]).then_inc(mean_ready, 1)
                        nc.vector.tensor_tensor(z_lo[:, g].rearrange("p (a b) n -> p a b n", a=2), z[:, :, :, 0:N],
                                                z_hi[:, g].rearrange("p (a b) n -> p a b n", a=2),
                                                ALU.subtract).then_inc(z_split, 1)
                    elif token == "M":
                        wait(dve, router_scored, i + 1)
                        nc.vector.tensor_tensor(score[:], router_ps[0:1, 0:G * E].rearrange("p (g e) -> p g e", g=G),
                                                rb[:].unsqueeze(1).to_broadcast([1, G, E]), ALU.add).then_inc(router_step, 1)
                        wait(dve, router_step, 4 * i + 1)
                        nc.vector.tensor_reduce(score_max[:], score[:], X, ALU.max).then_inc(router_step, 1)
                        wait(dve, router_step, 4 * i + 2)
                        nc.vector.tensor_tensor(best[:], score[:], score_max[:].unsqueeze(2).to_broadcast([1, G, E]),
                                                ALU.is_ge).then_inc(router_step, 1)
                        wait(dve, router_step, 4 * i + 3)
                        nc.vector.tensor_tensor(candidate[:], best[:], expert_less_e[:].unsqueeze(1).to_broadcast([1, G, E]),
                                                ALU.mult).then_inc(router_step, 1)
                        wait(dve, router_step, 4 * i + 4)
                        nc.vector.tensor_reduce(first[:], candidate[:], X, ALU.min).then_inc(first_ready, 1)
                        wait(dve, first_ready, i + 1)
                        nc.vector.tensor_scalar(top1[:, bass.ds(G * i, G)], first[:], float(E), float(E - 1), ALU.add,
                                                ALU.min).then_inc(routed, 1)

            run(dve, body)

            steps = 0

            def then_wait(instruction):
                nonlocal steps
                steps += 1
                instruction.then_inc(moment_step, 1)
                dve.wait_ge(moment_step, steps)

            dve.wait_ge(routed, GROUPS)
            for e in range(E):
                nc.vector.tensor_scalar(is_expert[:, e], top1[:], float(e), None, ALU.is_equal).then_inc(counted, 1)
            dve.wait_ge(counted, E)
            then_wait(nc.vector.tensor_reduce(count[:], is_expert[:], X, ALU.add))
            then_wait(nc.vector.tensor_scalar(count[:], count[:], float(N), 1.0, ALU.mult, ALU.max))
            nc.vector.reciprocal(inv_count1[:], count[:]).then_inc(count_ready, 1)
            dve.wait_ge(moments_made, 1)
            MOMENTS = 2 * E * KC
            then_wait(nc.vector.tensor_copy(inv_count[:], router_ps[:, MOMENTS:MOMENTS + E]))
            for t in range(2):
                last = nc.vector.tensor_tensor(
                    moment[:, t], router_ps[:, t * E * KC:(t + 1) * E * KC].rearrange("p (e c) -> p e c", e=E),
                    inv_count[:].unsqueeze(2).to_broadcast([128, E, KC]), ALU.mult)
            then_wait(last)
            then_wait(nc.vector.tensor_tensor(mean_sq[:], moment[:, 0], moment[:, 0], ALU.mult))
            then_wait(nc.vector.tensor_tensor(var[:], moment[:, 1], mean_sq[:], ALU.subtract))
            nc.vector.tensor_scalar(var[:], var[:], EPS, None, ALU.add).then_inc(var_all_ready, 1)
            dve.wait_ge(inv_std_ready, 1)
            then_wait(nc.vector.tensor_tensor(coef[:, 0], inv_std[:], gamma_sb[:], ALU.mult))
            then_wait(nc.vector.tensor_tensor(mean_sq[:], moment[:, 0], coef[:, 0], ALU.mult))
            nc.vector.tensor_tensor(coef[:, 1], beta_sb[:], mean_sq[:], ALU.subtract).then_inc(coef_ready, 1)
            for n in range(2 * E):
                dve.wait_ge(rows_made, n + 1)
                nc.vector.tensor_copy(coef_rows[:, n // E, n % E], out_ps[:, n % 2]).then_inc(rows_ready, 1)
            dve.wait_ge(rows_ready, 2 * E)

            LAG = 2

            def finish(n, s):
                dve.wait_ge(shifted, n + 1)
                nc.vector.scalar_tensor_tensor(out=x1_in[:, s], in0=out_sb[:, s], scalar=0.0, in1=x1_in[:, s],
                                               op0=ALU.max, op1=ALU.add).then_inc(y_ready, 1)

            with dve.Fori(0, B // SLOTS) as j:
                for s in range(SLOTS + LAG):
                    if s < SLOTS:
                        n = SLOTS * j + s
                        e = dve.value_load(top1[0:1, bass.ds(n, 1)], min_val=0, max_val=E - 1)
                        dve.wait_ge(slot_loaded[s], 32 * (j + 1))
                        nc.vector.tensor_tensor(out_sb[:, s], out_sb[:, s],
                                                coef_rows[:, 0, bass.ds(e, 1)].rearrange("p a f -> p (a f)"),
                                                ALU.mult).then_inc(scaled, 1)
                    if s >= LAG:
                        finish(SLOTS * j + s - LAG, s - LAG)

        @block.tensor
        def _(pe):
            pe.wait_ge(consts, 1)
            pe.wait_ge(const_loaded, 64)
            pe.wait_ge(ew_split, E)

            def body(i, mix, expert):
                for token, g in tokens(PE_ORDER, mix, expert):
                    if token == "J":
                        wait(pe, adj2_loaded, 16 * (i + 1))
                        wait(pe, adjT_ready, i)
                        for k in range(G):
                            last = nc.tensor.transpose(adjT_ps[:, k], adj_in2[:, k], ident[:])
                        last.then_inc(adj_transposed, 1)
                    elif token == "Z":
                        n = G * i + g
                        wait(pe, h2_ready, n + 1)
                        wait(pe, adjT_ready, i + 1)
                        wait(pe, z_split, n - 1)
                        for c in range(KC):
                            at = (c % 2) * (N + 1)
                            last = nc.tensor.matmul(z_ps[:, g % 2, c // 2, at:at + N + 1], h2[:, g, 128 * c:128 * c + 128],
                                                    adjT[:, g], start=True, stop=True)
                        last.then_inc(z_made, 1)
                    elif token == "M":
                        wait(pe, mean_ready, G * (i + 1))
                        wait(pe, routed, i)
                        for k in range(G):
                            for c in range(KC):
                                last = nc.tensor.matmul(router_ps[0:1, E * k:E * k + E], mean_h[:, k, c:c + 1], rw[:, c],
                                                        start=(c == 0), stop=(c == KC - 1))
                        last.then_inc(router_scored, 1)
                    elif token == "P":
                        n = G * (i - 1) + g
                        if g == 0:
                            wait(pe, routed, i)
                        e = pe.value_load(top1[0:1, bass.ds(n, 1)], min_val=0, max_val=E - 1)
                        wait(pe, z_split, n + 1)
                        wait(pe, squared, n - 1)

                        def of_expert(w, c):
                            return w[:, bass.ds(e, 1), c].rearrange("p a f -> p (a f)")

                        exact_product(nc, out_ps[:, g % 2], [z_hi[:, g, c] for c in range(KC)], [z_lo[:, g, c] for c in range(KC)],
                                      [of_expert(ew_hi, c) for c in range(KC)], [of_expert(ew_lo, c) for c in range(KC)]
                                      ).then_inc(out_made, 1)

            run(pe, body)

            pe.wait_ge(summed, B)
            pe.wait_ge(count_ready, 1)
            pe.wait_ge(routed, GROUPS)
            for t in range(2):
                for e in range(E):
                    for c in range(KC):
                        at = (t * E + e) * KC + c
                        nc.tensor.matmul(router_ps[:, at:at + 1], sums[:, t, e, 128 * c:128 * c + 128], ones[:, 0:1],
                                         start=True, stop=True)
            MOMENTS = 2 * E * KC
            nc.tensor.matmul(router_ps[:, MOMENTS:MOMENTS + E], ones[0:1, :], inv_count1[:],
                             start=True, stop=True).then_inc(moments_made, 1)
            pe.wait_ge(coef_ready, 1)
            for n in range(2 * E):
                if n >= 2:
                    pe.wait_ge(rows_ready, n - 1)
                for c in range(KC):
                    last = nc.tensor.transpose(out_ps[:, n % 2, 128 * c:128 * c + 128],
                                               coef[:, n // E, n % E, c:c + 1].to_broadcast([128, 128]), ident[:])
                last.then_inc(rows_made, 1)


def program(nc, x, adj, wq, wk, wv, wo, router_w, router_b, expert_w, gamma, beta, y):
    B, N, D = x.shape
    x1_dram = nc.dram_tensor("x1_dram", [B, N, D], F32, kind="Internal").ap()
    out_dram = nc.dram_tensor("out_dram", [B, N, D], F32, kind="Internal").ap()
    with ExitStack() as outer:
        def sem(name):
            return outer.enter_context(nc.semaphore(name))

        ident = outer.enter_context(nc.sbuf_tensor("ident", [128, 128], F32))
        ident_step = sem("ident_step")
        with nc.Block() as block:

            @block.gpsimd
            def _(pool):
                nc.gpsimd.memset(ident[:], 0.0).then_inc(ident_step, 1)
                pool.wait_ge(ident_step, 1)
                nc.gpsimd.affine_select(out=ident[:], in_=ident[:], compare_op=ALU.not_equal, fill=1.0, base=0,
                                        pattern=[[-1, 128]], channel_multiplier=1).then_inc(ident_step, 1)
                pool.wait_ge(ident_step, 2)

        with ExitStack() as ctx:
            attention_layer(nc, ctx, sem, ident, x, adj, (wq, wk, wv, wo), x1_dram)
        with ExitStack() as ctx:
            expert_layer(nc, ctx, sem, ident, x1_dram, adj, router_w, router_b, expert_w, gamma, beta, out_dram, y)


def kernel(x, adj, L0_gnn_Wq, L0_gnn_Wk, L0_gnn_Wv, L0_gnn_Wo, L1_gnn_router_w, L1_gnn_router_b, L1_gnn_expert_w,
           L1_gnn_bn_gamma, L1_gnn_bn_beta):
    import numpy as np
    import concourse.bacc as bacc
    from concourse.bass_utils import run_bass_kernel_spmd

    E, D = np.shape(L1_gnn_bn_gamma)
    C = D // 128

    def by_feature(a):
        return np.asarray(a).reshape(E, C, 128).transpose(2, 0, 1)

    inputs = {
        "x": x,
        "adj": adj,
        "wq": np.asarray(L0_gnn_Wq).T,
        "wk": np.asarray(L0_gnn_Wk).T,
        "wv": np.asarray(L0_gnn_Wv).T,
        "wo": np.asarray(L0_gnn_Wo).T,
        "router_w": np.asarray(L1_gnn_router_w).reshape(C, 128, E).transpose(1, 0, 2),
        "router_b": np.asarray(L1_gnn_router_b).reshape(1, E),
        "expert_w": L1_gnn_expert_w,
        "gamma": by_feature(L1_gnn_bn_gamma),
        "beta": by_feature(L1_gnn_bn_beta),
    }
    arrays = {f"in_{name}": np.ascontiguousarray(a) for name, a in inputs.items()}
    nc = bacc.Bacc("TRN2", target_bir_lowering=False, num_devices=1)
    args = [nc.dram_tensor(name, a.shape, mybir.dt.from_np(a.dtype), kind="ExternalInput").ap() for name, a in arrays.items()]
    y = nc.dram_tensor("y", np.shape(x), F32, kind="ExternalOutput").ap()
    program(nc, *args, y)
    return run_bass_kernel_spmd(nc, [arrays], core_ids=[0]).results[0]["y"]
```

```python
from contextlib import ExitStack

import concourse.bass as bass
from concourse import mybir

F32 = mybir.dt.float32
F32R = mybir.dt.float32r
I32 = mybir.dt.int32
ALU = mybir.AluOpType
ACT = mybir.ActivationFunctionType
X = mybir.AxisListType.X

HEADS = 16
EPS = 1e-5


def wait(engine, semaphore, value):
    if not isinstance(value, int) or value > 0:
        engine.wait_ge(semaphore, value)


def exact_product(nc, out, a_hi, a_lo, b_hi, b_lo):
    terms = [t for k in range(len(a_hi)) for t in ((a_hi[k], b_hi[k]), (a_hi[k], b_lo[k]), (a_lo[k], b_hi[k]))]
    for n, (a, b) in enumerate(terms):
        last = nc.tensor.matmul(out, a, b, start=(n == 0), stop=(n == len(terms) - 1))
    return last


def keep_clock_up(nc, pe, out, ident, transposes):
    with pe.Fori(0, transposes // 4):
        for _ in range(4):
            nc.tensor.transpose(out, ident[:], ident[:])


def halves_combined(nc, bn, mean_sum, mean_diff, m2):
    nc.vector.tensor_tensor(mean_sum[:], bn[:, :, 1], bn[:, :, 4], ALU.add)
    nc.vector.tensor_tensor(mean_diff[:], bn[:, :, 1], bn[:, :, 4], ALU.subtract)
    return nc.vector.tensor_tensor(m2[:], bn[:, :, 2], bn[:, :, 5], ALU.add)


def scaled_moments(nc, count, mean_sum, mean_diff, m2, neg_mean):
    nc.vector.tensor_scalar(neg_mean[:], mean_sum[:], -0.5, None, ALU.mult)
    nc.vector.tensor_tensor(mean_diff[:], mean_diff[:], mean_diff[:], ALU.mult)
    return nc.vector.tensor_scalar(m2[:], m2[:], 1.0 / count, EPS, ALU.mult, ALU.add)


def attention_layer(nc, ctx, sem, ident, x, adj, weights, x1_dram, expert_w, shared):
    w_hi, w_raw, w_raw_loaded, ew_hi_ready, ew_split, x1_in, x1_loaded = shared
    B, N, D = x.shape
    PAIRS = B // 2
    KC = D // 128
    R = 4
    C = HEADS // R
    HD = D // HEADS
    STEPS = 2 * C
    SCALE = float(D) ** -0.5
    STACKS = 16 * 3 * R

    def sb(name, shape, dt=F32):
        return ctx.enter_context(nc.sbuf_tensor(name, shape, dt))

    def ps(name, shape):
        return ctx.enter_context(nc.psum_tensor(name, shape, F32))

    w_lo = sb("w_lo", [N, 4, KC, D], F32R)
    x_in, h = x1_in[:, 0:2], x1_in[:, 2:4]
    hT_hi = sb("hT_hi", [128, KC, 2, N], F32R)
    hT_lo = sb("hT_lo", [128, KC, 2, N], F32R)
    Q_LO, Q_HI, K_HI, K_LO = range(4)
    qk = sb("qk", [128, 4, 2, C, N], F32R)
    stack = sb("stack", [3 * HD, 2, R, 2, C, N], F32R)
    v = sb("v", [N, 2, D])
    logits = sb("logits", [N, 4, R, N])
    prob = sb("prob", [N, 4, R, N])
    probT = sb("probT", [N, 4, R, N])
    o_hi = sb("o_hi", [128, C, N], F32R)
    o_lo = sb("o_lo", [128, C, N], F32R)
    x_res = sb("x_res", [N, 2, D])
    adj_in = sb("adj_in", [N, 2, N])
    adj2 = sb("adj2", [N, 2, N])
    bn = sb("bn", [N, 2, 6])
    mean_sum = sb("mean_sum", [N, 2])
    mean_diff = sb("mean_diff", [N, 2])
    m2 = sb("m2", [N, 2])
    var_eps = sb("var_eps", [N, 2])
    neg_mean = sb("neg_mean", [N, 2])
    minus_half = sb("minus_half", [N, 2])
    rstd = sb("rstd", [N, 2])
    shift = sb("shift", [N, 2])
    neg_max = sb("neg_max", [N, 4, R])
    abs_max = sb("abs_max", [N, 4, R])
    row_sum = sb("row_sum", [N, 4, R])
    inv_sum = sb("inv_sum", [N, 4, R])
    norm = sb("norm", [N, 4, R])

    scores_ps = ps("scores_ps", [N, 2, R, N])
    probT_ps = ps("probT_ps", [N, 2, R, N])
    o_ps = ps("o_ps", [128, C, N])
    bank = ps("bank", [128, 3, 512])

    w_loaded = [sem(f"w_loaded{n}") for n in range(4)]
    w_hi_ready, w_split = sem("w_hi_ready"), sem("w_split")
    x_loaded, var_ready, rstd_ready, shift_ready, h_ready = map(
        sem, ("x_loaded", "var_ready", "rstd_ready", "shift_ready", "h_ready"))
    bn_done, halves_done, scaled_done = sem("bn_done"), sem("halves_done"), sem("scaled_done")
    h_transposed, hT_hi_ready, hT_split = sem("h_transposed"), sem("hT_hi_ready"), sem("hT_split")
    qk_projected, qk_hi_ready, qk_split = sem("qk_projected"), sem("qk_hi_ready"), sem("qk_split")
    stacked = [sem("stacked0"), sem("stacked1")]
    v_projected, v_copied = sem("v_projected"), sem("v_copied")
    adj_loaded, adj_doubled = sem("adj_loaded"), sem("adj_doubled")
    scored, logits_ready, neg_max_ready, abs_max_ready = map(
        sem, ("scored", "logits_ready", "neg_max_ready", "abs_max_ready"))
    exp_done, inverted, norm_ready, normed = map(sem, ("exp_done", "inverted", "norm_ready", "normed"))
    transposed, probT_ready, applied = sem("transposed"), sem("probT_ready"), sem("applied")
    o_hi_ready, o_split, o_projected = sem("o_hi_ready"), sem("o_split"), sem("o_projected")
    x_res_loaded = [sem("x_res_loaded0"), sem("x_res_loaded1")]
    x1_ready = sem("x1_ready")
    x1_stored = [sem("x1_stored0"), sem("x1_stored1")]
    half_ready = sem("half_ready")

    PE_ORDER = """S0 W5' T6' H1' O0'
                  S1 T7' W6' Q0
                  S2 T0 W7' Q1
                  S3 T1 W0 Q2
                  S4 W1 T2 Q3
                  S5 T3 W2 O1'
                  S6 T4 W3 V0
                  S7 T5 W4 H0 V1"""
    ACT_ORDER = """H1' C6' E0
                   C7' E1
                   C0 Q0 O1' E2
                   V1' Q1 C1 E3
                   Q2 C2 E4
                   Q3 C3 E5
                   C4 A0 O0 E6
                   A1 V0 C5 H0 E7"""
    DVE_ORDER = """R7' L0 H1' B0
                   N0 R0 L1 X0' B1
                   N1 L2 R1 Q0 O1' B2
                   R2 L3 Q1 B3
                   M R3 L4 Q2 B4
                   R4 Q3 L5 B5
                   L6 R5 X1' B6
                   O0 R6 L7 H0 B7"""
    POOL_ORDER = "P7' D1' P0 P1 P2 P3 G P4 D0 P5 P6"
    SP_ORDER = "X K1' J Z1' Y0' Z0 K0 Y1'"
    AHEAD = {"sp": dict(X=2, J=1, K=1), "pe": dict(Q=1, V=1, H=2), "act": dict(Q=1, V=1, H=2, A=2),
             "dve": dict(Q=1, H=2, N=2, M=2), "pool": dict(G=2, D=1)}
    START = {("act", -2): "U0 A0 A1 H0", ("act", -1): "H1' U1 U2 Q0 Q1 U3 Q2 Q3 A0 A1 V0 H0",
             ("dve", -2): "N0 N1 M U0 H0", ("dve", -1): "H1' U1 U2 N0 N1 Q0 Q1 U3 M Q2 Q3 H0",
             ("sp", 0): "X K1' J Z1' Y0' Z0 W K0 Y1'",
             ("sp", PAIRS - 1): "K1' F Z1' Y0' Z0 Y1'",
             ("act", PAIRS): "C6' F0 C7' O1' F1", ("dve", PAIRS): "R7' F0 X0' O1' X1' F1"}
    Q_BANK, V_BANK, O_BANK, H_BANK = (2, 1, 0, 2), (2, 0), (1, 1), (1, 2)

    def tokens(engine, order, i):
        for t in (START.get((engine, i), order) if isinstance(i, int) else order).split():
            pair = 0 if t[0] in "UF" else i + (AHEAD[engine].get(t[0], 0) - t.endswith("'"))
            if not isinstance(pair, int) or 0 <= pair < PAIRS:
                yield t[0], int(t[1:].strip("'") or 0), pair

    def raw_weights(n):
        return (logits, prob, probT)[n % 3][:].rearrange("p k r n -> p k (r n)")

    def exists(pair):
        return not isinstance(pair, int) or pair < PAIRS

    def run(engine, body):
        for i in (-2, -1, 0, 1):
            body(i)
        with engine.Fori(2, PAIRS - 2) as i:
            body(i)
        for i in (PAIRS - 2, PAIRS - 1, PAIRS):
            body(i)

    with nc.Block() as block:

        @block.sync
        def _(sp):
            sp.dma_start(x_in[:], x[0:2].rearrange("g n f -> n g f")).then_inc(x_loaded, 16)
            for n, w in enumerate(weights):
                if n >= 3:
                    sp.wait_ge(w_split, n - 2)
                sp.dma_start(raw_weights(n), w.rearrange("(k p) f -> p k f", p=128)).then_inc(w_loaded[n], 16)

            def body(i):
                for token, g, j in tokens("sp", SP_ORDER, i):
                    if token == "F":
                        for place in range(2):
                            sp.wait_ge(h_transposed, 2 * PAIRS)
                            sp.dma_start(x1_in[:, 2 * place:2 * place + 2], x1_dram[2 * place:2 * place + 2].rearrange("g n f -> n g f")).then_inc(x1_loaded[place], 16)
                    elif token == "W":
                        for e, loaded in enumerate(w_raw_loaded):
                            sp.dma_start(w_raw[:, e].bitcast(F32), expert_w[e].rearrange("(k p) f -> p k f", p=128)).then_inc(loaded, 16)
                    elif token == "X" and not (isinstance(j, int) and j == 0):
                        wait(sp, h_ready, 2 * j)
                        sp.dma_start(x_in[:], x[bass.ds(2 * j, 2)].rearrange("g n f -> n g f")).then_inc(x_loaded, 16)
                    elif token == "J":
                        wait(sp, adj_doubled, 2 * j)
                        sp.dma_start(adj_in[:], adj[bass.ds(2 * j, 2)].rearrange("g n m -> n g m")).then_inc(adj_loaded, 16)
                    elif token == "Z":
                        wait(sp, x1_stored[g], 16 * j)
                        sp.dma_start(x_res[:, g, :], x[bass.ds(2 * j + g, 1)].rearrange("g n f -> n (g f)")).then_inc(x_res_loaded[g], 16)
                    elif token == "Y":
                        wait(sp, x1_ready, 2 * j + g + 1)
                        sp.dma_start(x1_dram[bass.ds(2 * j + g, 1)].rearrange("g n f -> n (g f)"), x_res[:, g, :]).then_inc(x1_stored[g], 16)
                    elif token == "K":
                        wait(sp, qk_split, 4 * (j + 1))
                        wait(sp, scored, STEPS * (j - 1) + C * (g + 1))
                        for s, (a, b) in enumerate(((Q_HI, K_HI), (Q_LO, K_HI), (Q_HI, K_LO))):
                            for r in range(R):
                                sp.dma_start(
                                    stack[HD * s:HD * s + HD, g, r].bitcast(F32).rearrange("p t c n -> p t (c n)"),
                                    qk[HD * r:HD * r + HD, a:b + 1:b - a, g].bitcast(F32).rearrange("p t c n -> p t (c n)"),
                                ).then_inc(stacked[g], 16)

            run(sp, body)
            for g in range(2):
                sp.wait_ge(x1_stored[g], 16 * PAIRS)

        @block.gpsimd
        def _(pool):
            nc.gpsimd.memset(minus_half[:], -0.5).then_inc(half_ready, 1)
            pool.wait_ge(half_ready, 1)

            def body(i):
                for token, k, j in tokens("pool", POOL_ORDER, i):
                    if token == "P":
                        slot = k % 4
                        wait(pool, norm_ready, STEPS * j + k + 1)
                        nc.gpsimd.tensor_tensor(prob[:, slot], prob[:, slot],
                                                norm[:, slot].unsqueeze(2).to_broadcast([N, R, N]),
                                                ALU.mult).then_inc(normed, 1)
                    elif token == "G":
                        wait(pool, var_ready, j + 1)
                        wait(pool, h_ready, 2 * j)
                        nc.gpsimd.tensor_tensor(rstd[:], var_eps[:], minus_half[:], ALU.pow).then_inc(rstd_ready, 1)
                        wait(pool, rstd_ready, j + 1)
                        nc.gpsimd.tensor_tensor(shift[:], neg_mean[:], rstd[:], ALU.mult).then_inc(shift_ready, 1)
                    elif token == "D":
                        wait(pool, adj_loaded, 16 * (j + 1))
                        wait(pool, logits_ready, STEPS * (j - 1) + C * (k + 1))
                        nc.gpsimd.tensor_tensor(adj2[:, k], adj_in[:, k], adj_in[:, k], ALU.add).then_inc(adj_doubled, 1)

            run(pool, body)

        @block.scalar
        def _(act):
            def body(i):
                for token, k, j in tokens("act", ACT_ORDER, i):
                    slot = k % 4
                    if token == "U":
                        act.wait_ge(w_loaded[k], 16)
                        nc.scalar.activation(w_hi[:, k], raw_weights(k), ACT.Copy).then_inc(w_hi_ready, 1)
                    elif token == "F":
                        act.wait_ge(qk_projected, 4 * PAIRS)
                        act.wait_ge(v_projected, 2 * PAIRS)
                        act.wait_ge(w_raw_loaded[k], 16)
                        nc.scalar.activation(w_hi[:, k], w_raw[:, k].bitcast(F32), ACT.Copy).then_inc(ew_hi_ready, 1)
                    elif token == "E":
                        wait(act, neg_max_ready, STEPS * j + k + 1)
                        wait(act, transposed, STEPS * j + k - 3)
                        for r in range(R):
                            last = nc.scalar.activation(prob[:, slot, r], logits[:, slot, r], ACT.Exp,
                                                        bias=neg_max[:, slot, r:r + 1],
                                                        accum_out=row_sum[:, slot, r:r + 1])
                        last.then_inc(exp_done, 1)
                    elif token == "C":
                        wait(act, transposed, STEPS * j + k + 1)
                        wait(act, applied, STEPS * j + k - 3)
                        nc.scalar.activation(probT[:, slot], probT_ps[:, k % 2], ACT.Copy).then_inc(probT_ready, 1)
                    elif token == "O":
                        wait(act, applied, STEPS * j + C * (k + 1))
                        wait(act, o_projected, 2 * j + k)
                        nc.scalar.activation(o_hi[:], o_ps[:], ACT.Copy).then_inc(o_hi_ready, 1)
                    elif token == "Q":
                        wait(act, qk_projected, 4 * j + k + 1)
                        if k == 0:
                            for g in range(2):
                                wait(act, stacked[g], STACKS * j)
                        t, c = (Q_HI, K_HI)[k // 2], 2 * (k % 2)
                        nc.scalar.activation(qk[:, t, :, c:c + 2].rearrange("p g c n -> p c g n"),
                                             bank[:, Q_BANK[k]].rearrange("p (c g n) -> p c g n", c=2, g=2),
                                             ACT.Copy).then_inc(qk_hi_ready, 1)
                    elif token == "V":
                        wait(act, v_projected, 2 * j + k + 1)
                        wait(act, applied, STEPS * (j - 1) + C * (k + 1))
                        nc.scalar.activation(v[:, k], bank[:, V_BANK[k]], ACT.Copy).then_inc(v_copied, 1)
                    elif token == "A":
                        wait(act, shift_ready, j + 1)
                        wait(act, h_transposed, 2 * (j - 1) + k + 1)
                        nc.scalar.activation(h[:, k], x_in[:, k], ACT.Relu, bias=shift[:, k:k + 1],
                                             scale=rstd[:, k:k + 1]).then_inc(h_ready, 1)
                    elif token == "H":
                        wait(act, h_transposed, 2 * j + k + 1)
                        nc.scalar.activation(hT_hi[:, :, k], bank[:, H_BANK[k]].rearrange("p (c n) -> p c n", n=N),
                                             ACT.Copy).then_inc(hT_hi_ready, 1)

            run(act, body)

        @block.vector
        def _(dve):
            def body(i):
                for token, k, j in tokens("dve", DVE_ORDER, i):
                    slot = k % 4
                    if token == "U":
                        dve.wait_ge(w_hi_ready, k + 1)
                        nc.vector.tensor_tensor(w_lo[:, k], raw_weights(k), w_hi[:, k], ALU.subtract).then_inc(w_split, 1)
                    elif token == "F":
                        dve.wait_ge(ew_hi_ready, k + 1)
                        nc.vector.tensor_tensor(w_raw[:, k], w_raw[:, k].bitcast(F32), w_hi[:, k], ALU.subtract).then_inc(ew_split, 1)
                    elif token == "L":
                        wait(dve, scored, STEPS * j + k + 1)
                        wait(dve, exp_done, STEPS * j + k - 3)
                        if k % C == 0:
                            wait(dve, adj_doubled, 2 * j + k // C + 1)
                            if isinstance(j, int) and j == 0:
                                dve.wait_ge(w_split, 4)
                        nc.vector.scalar_tensor_tensor(
                            out=logits[:, slot], in0=scores_ps[:, k % 2], scalar=SCALE,
                            in1=adj2[:, k // C].unsqueeze(1).to_broadcast([N, R, N]),
                            op0=ALU.mult, op1=ALU.add).then_inc(logits_ready, 1)
                        wait(dve, logits_ready, STEPS * j + k + 1)
                        nc.vector.tensor_reduce(neg_max[:, slot], logits[:, slot], X, ALU.max,
                                                negate=True).then_inc(neg_max_ready, 1)
                    elif token == "B":
                        nc.vector.tensor_reduce(abs_max[:, slot], logits[:, slot], X, ALU.max,
                                                apply_absolute_value=True).then_inc(abs_max_ready, 1)
                    elif token == "R":
                        wait(dve, exp_done, STEPS * j + k + 1)
                        wait(dve, abs_max_ready, STEPS * j + k + 1)
                        nc.vector.reciprocal(inv_sum[:, slot], row_sum[:, slot]).then_inc(inverted, 1)
                        wait(dve, inverted, STEPS * j + k + 1)
                        wait(dve, normed, STEPS * j + k - 3)
                        nc.vector.scalar_tensor_tensor(
                            out=norm[:, slot], in0=abs_max[:, slot], scalar=0.0, in1=inv_sum[:, slot],
                            op0=ALU.not_equal, op1=ALU.mult).then_inc(norm_ready, 1)
                    elif token == "O":
                        wait(dve, o_hi_ready, 2 * j + k + 1)
                        nc.vector.tensor_tensor(o_lo[:], o_ps[:], o_hi[:], ALU.subtract).then_inc(o_split, 1)
                    elif token == "X":
                        wait(dve, o_projected, 2 * j + k + 1)
                        wait(dve, x_res_loaded[k], 16 * (j + 1))
                        nc.vector.tensor_tensor(x_res[:, k], bank[:, O_BANK[k]], x_res[:, k],
                                                ALU.add).then_inc(x1_ready, 1)
                    elif token == "Q":
                        wait(dve, qk_hi_ready, 4 * j + k + 1)
                        hi, lo = ((Q_HI, Q_LO), (K_HI, K_LO))[k // 2]
                        c = 2 * (k % 2)
                        nc.vector.tensor_tensor(qk[:, lo, :, c:c + 2].rearrange("p g c n -> p c g n"),
                                                bank[:, Q_BANK[k]].rearrange("p (c g n) -> p c g n", c=2, g=2),
                                                qk[:, hi, :, c:c + 2].rearrange("p g c n -> p c g n"),
                                                ALU.subtract).then_inc(qk_split, 1)
                    elif token == "N":
                        wait(dve, x_loaded, 16 * (j + 1))
                        nc.vector.bn_stats(bn[:, k], x_in[:, k]).then_inc(bn_done, 1)
                    elif token == "M":
                        wait(dve, bn_done, 2 * (j + 1))
                        halves_combined(nc, bn, mean_sum, mean_diff, m2).then_inc(halves_done, 1)
                        wait(dve, halves_done, j + 1)
                        wait(dve, shift_ready, j)
                        scaled_moments(nc, D, mean_sum, mean_diff, m2, neg_mean).then_inc(scaled_done, 1)
                        wait(dve, scaled_done, j + 1)
                        nc.vector.scalar_tensor_tensor(out=var_eps[:], in0=mean_diff[:], scalar=0.25, in1=m2[:],
                                                       op0=ALU.mult, op1=ALU.add).then_inc(var_ready, 1)
                    elif token == "H":
                        wait(dve, hT_hi_ready, 2 * j + k + 1)
                        nc.vector.tensor_tensor(hT_lo[:, :, k], bank[:, H_BANK[k]].rearrange("p (c n) -> p c n", n=N),
                                                hT_hi[:, :, k], ALU.subtract).then_inc(hT_split, 1)

            run(dve, body)

        @block.tensor
        def _(pe):
            def body(i):
                for token, k, j in tokens("pe", PE_ORDER, i):
                    g, c, slot = k // C, k % C, k % 4
                    if token == "S":
                        if c == 0:
                            wait(pe, stacked[g], STACKS * (j + 1))
                        wait(pe, logits_ready, STEPS * j + k - 1)
                        for r in range(R):
                            last = nc.tensor.matmul(scores_ps[:, k % 2, r], stack[:, g, r, 0, c], stack[:, g, r, 1, c],
                                                    start=True, stop=True)
                        last.then_inc(scored, 1)
                    elif token == "T":
                        wait(pe, normed, STEPS * j + k + 1)
                        wait(pe, probT_ready, STEPS * j + k - 1)
                        for r in range(R):
                            last = nc.tensor.transpose(probT_ps[:, k % 2, r], prob[:, slot, r], ident[:])
                        last.then_inc(transposed, 1)
                    elif token == "W":
                        wait(pe, probT_ready, STEPS * j + k + 1)
                        if c == 0:
                            wait(pe, v_copied, 2 * j + g + 1)
                            wait(pe, o_split, 2 * j + g)
                        for r in range(R):
                            f = HD * (R * c + r)
                            last = nc.tensor.matmul(o_ps[HD * r:HD * r + HD, c], v[:, g, f:f + HD], probT[:, slot, r],
                                                    start=True, stop=True)
                        last.then_inc(applied, 1)
                    elif token == "O":
                        wait(pe, o_split, 2 * j + k + 1)
                        if isinstance(j, int) and j == 0 and k == 0:
                            pe.wait_ge(w_split, 4)
                        if exists(j + 2):
                            wait(pe, *((hT_split, 2 * (j + 2) + 1), (qk_split, 4 * (j + 2) + 2))[k])
                        else:
                            wait(pe, x1_ready, 2 * j + k)
                        exact_product(nc, bank[:, O_BANK[k]], [o_hi[:, c] for c in range(C)], [o_lo[:, c] for c in range(C)],
                                      [w_hi[:, 3, c] for c in range(C)], [w_lo[:, 3, c] for c in range(C)]
                                      ).then_inc(o_projected, 1)
                    elif token == "Q":
                        if isinstance(j, int) and j == 0 and k % 2 == 0:
                            pe.wait_ge(w_split, k // 2 + 1)
                        wait(pe, *((hT_split, 2 * (j + 1)), (x1_ready, 2 * (j - 2) + 1), (v_copied, 2 * j),
                                   (qk_split, 4 * j + 1))[k])
                        for half in range(2):
                            m = 128 * (2 * (k % 2) + half)
                            last = exact_product(nc, bank[:, Q_BANK[k], 256 * half:256 * half + 256],
                                                 [w_hi[:, k // 2, kc, m:m + 128] for kc in range(KC)],
                                                 [w_lo[:, k // 2, kc, m:m + 128] for kc in range(KC)],
                                                 [hT_hi[:, kc] for kc in range(KC)], [hT_lo[:, kc] for kc in range(KC)])
                        last.then_inc(qk_projected, 1)
                    elif token == "V":
                        if isinstance(j, int) and j == 0 and k == 0:
                            pe.wait_ge(w_split, 3)
                        wait(pe, qk_split, 4 * j + (4, 3)[k])
                        exact_product(nc, bank[:, V_BANK[k]], [hT_hi[:, kc, k] for kc in range(KC)],
                                      [hT_lo[:, kc, k] for kc in range(KC)],
                                      [w_hi[:, 2, kc] for kc in range(KC)], [w_lo[:, 2, kc] for kc in range(KC)]
                                      ).then_inc(v_projected, 1)
                    elif token == "H":
                        wait(pe, h_ready, 2 * j + k + 1)
                        wait(pe, *((x1_ready, 2 * (j - 2)), (v_copied, 2 * (j - 1) + 1))[k])
                        for kc in range(KC):
                            last = nc.tensor.transpose(bank[:, H_BANK[k], 128 * kc:128 * kc + 128],
                                                       h[:, k, 128 * kc:128 * kc + 128], ident[:])
                        last.then_inc(h_transposed, 1)

            keep_clock_up(nc, pe, bank[:, 0, 0:128], ident, 40)
            run(pe, body)


def expert_layer(nc, ctx, sem, ident, x1_dram, adj, router_w, router_b, gamma, beta, out_dram, y, shared):
    ew_hi, w_raw, w_raw_loaded, ew_hi_ready, ew_split, x1_in, x1_loaded = shared
    B, N, D = x1_dram.shape
    E = w_raw.shape[1]
    KC = D // 128
    G = 4
    GROUPS = B // G
    STORED = GROUPS // 2

    def sb(name, shape, dt=F32):
        return ctx.enter_context(nc.sbuf_tensor(name, shape, dt))

    def ps(name, shape):
        return ctx.enter_context(nc.psum_tensor(name, shape, F32))

    ew_lo = w_raw
    h2 = sb("h2", [N, G, D])
    outs = sb("outs", [N, G * (1 + GROUPS - STORED), D])
    square = sb("square", [N, G, D])
    adj_in2 = sb("adj_in2", [N, G, N])
    adjT = sb("adjT", [N, G, N + 1])
    z_hi = sb("z_hi", [128, G, KC, N], F32R)
    z_lo = sb("z_lo", [128, G, KC, N], F32R)
    mean_h = sb("mean_h", [128, G, KC])
    sums = sb("sums", [N, 2, E, D])
    rw = sb("rw", [128, KC, E])
    rb = sb("rb", [1, E])
    expert_less_e = sb("expert_less_e", [1, E])
    score = sb("score", [1, G, E])
    score_max = sb("score_max", [1, G])
    best = sb("best", [1, G, E])
    candidate = sb("candidate", [1, G, E])
    first = sb("first", [1, G])
    top1 = sb("top1", [1, B], I32)
    bn = sb("bn2", [N, G, 6])
    mean_sum = sb("mean_sum2", [N, G])
    mean_diff = sb("mean_diff2", [N, G])
    m2 = sb("m22", [N, G])
    var_eps = sb("var_eps2", [N, G])
    neg_mean = sb("neg_mean2", [N, G])
    minus_half = sb("minus_half2", [N, E * KC])
    rstd = sb("rstd2", [N, G])
    shift = sb("shift2", [N, G])
    ones = sb("ones", [N, 128])
    gamma_sb = sb("gamma_sb", [128, E, KC])
    beta_sb = sb("beta_sb", [128, E, KC])
    is_expert = sb("is_expert", [1, E, B])
    count = sb("count", [1, E])
    inv_count1 = sb("inv_count1", [1, E])
    inv_count = sb("inv_count", [128, E])
    moment = sb("moment", [128, 2, E, KC])
    mean_sq = sb("mean_sq", [128, E, KC])
    var = sb("var", [128, E, KC])
    inv_std = sb("inv_std", [128, E, KC])
    coef = sb("coef", [128, 2, E, KC])
    coef_rows = (x1_in, h2)
    assert KC == G
    x1_store = ew_hi[:].bitcast(F32), w_raw[:].bitcast(F32)

    adjT_ps = ps("adjT_ps", [N, G, N])
    router_ps = ps("router_ps", [128, 512])
    z_ps = ps("z_ps", [128, 2, 2, 512])
    out_ps = ps("out_ps", [N, 2, D])

    const_loaded, consts, adj2_loaded = sem("const_loaded"), sem("consts"), sem("adj2_loaded")
    bn_done, halves_done, scaled_done, var_ready, rstd_ready, shift_ready, h2_ready = map(
        sem, ("bn_done2", "halves_done2", "scaled_done2", "var_ready2", "rstd_ready2", "shift_ready2", "h2_ready"))
    adj_transposed, adjT_ready = sem("adj_transposed"), sem("adjT_ready")
    z_made, z_hi_ready, mean_ready, z_split = map(sem, ("z_made", "z_hi_ready", "mean_ready", "z_split"))
    router_scored, router_step, first_ready, routed = map(sem, ("router_scored", "router_step", "first_ready", "routed"))
    out_made, out_copied, squared, summed, square_summed = map(
        sem, ("out_made", "out_copied", "squared", "summed", "square_summed"))
    out_stored = [sem(f"out_stored{g}") for g in range(G)]
    counted, count_ready, inv_count_made, sums_transposed, moment_summed, moment_step = map(
        sem, ("counted", "count_ready", "inv_count_made", "sums_transposed", "moment_summed", "moment_step"))
    var_all_ready, inv_std_ready, coef_ready, rows_made = map(
        sem, ("var_all_ready", "inv_std_ready", "coef_ready", "rows_made"))
    rows_ready = [sem("rows0_ready"), sem("rows1_ready")]

    PE_ORDER = "Z0 Z1 J P0 P1 Z2 P2 Z3 P3 M"
    ACT_ORDER = "A2' A3' Z0 P0 A0 A1 Z1 P1 Z2 P2 Z3 P3"
    DVE_ORDER = "M' Y0 Y1 S3' N0 Z0 S0 Z1 S1 Y2 N1 Z2 S2 Y3 J Z3"
    POOL_ORDER = "N0 P0 N1 P1 P2 P3"
    SP_ORDER = "X1 P0 X0 P1 J P2 P3"
    AHEAD = {"sp": {"X0": 2, "X1": 1, "J": 2, "P": -1}, "pe": {"J": 1, "P": -1}, "act": {"A": 1, "P": -1},
             "dve": {"N": 1, "J": 1, "S": -1}, "pool": {"N": 1, "P": -1}}

    START = {("act", -1): "A0 A1 U2", ("act", 0): "A2' A3' Z0 Z1 Z2 Z3 A0 A1 U3",
             ("dve", -1): "N0 N1 J U2", ("dve", 0): "Y0 Y1 Z0 Z1 N0 Y2 Y3 Z2 J Z3",
             ("dve", 1): "M' N1' Y0 Y1 U3 N0 Z0 S0 Z1 S1 Y2 N1 Z2 S2 Y3 J Z3"}

    def tokens(engine, order, i):
        ahead = AHEAD[engine]
        for t in (START.get((engine, i), order) if isinstance(i, int) else order).split():
            group = 0 if t[0] == "U" else i + (ahead.get(t, ahead.get(t[0], 0)) - t.endswith("'"))
            if not isinstance(group, int) or 0 <= group < GROUPS:
                yield t[0], int(t[1:].strip("'") or 0), group

    def run(engine, body):
        for i in (-2, -1, 0, 1, 2):
            body(i, False)
        with engine.Fori(3, STORED + 1) as i:
            body(i, False)
        body(STORED + 1, True)
        with engine.Fori(STORED + 2, GROUPS - 2) as i:
            body(i, True)
        for i in (GROUPS - 2, GROUPS - 1, GROUPS, GROUPS + 1):
            body(i, True)

    def out_of(group, g, stays):
        return outs[:, bass.ds(G * (group - STORED + 1) + g, 1)].rearrange("p a f -> p (a f)") if stays else outs[:, g]

    CHUNKS = B // G
    RING = 4
    assert CHUNKS - STORED == 2 * RING == 2 * E == STORED
    x1_chunk_loaded = [sem(f"x1_chunk_loaded{s}") for s in range(RING)]
    out_chunk_loaded = [sem(f"out_chunk_loaded{s}") for s in range(RING)]
    ROUNDS = (CHUNKS - STORED) // RING
    y_stored = [sem(f"y_stored{p}") for p in range(CHUNKS - STORED)]
    scaled, shifted, y_ready = sem("scaled"), sem("shifted"), sem("y_ready")

    def for_rounds(engine, round_of):
        with engine.Fori(0, ROUNDS) as n:
            round_of(n, True)
        with engine.Fori(ROUNDS, CHUNKS // RING) as n:
            round_of(n, False)

    def graph_of(n, s, g, stayed):
        return G * (RING * n + s) + g + (G * STORED if stayed else -G * RING * ROUNDS)

    def x1_chunk(n, s, stayed):
        half = RING // 2
        return x1_store[s // half][:, bass.ds(half * n + s % half - (0 if stayed else half * ROUNDS), 1)]

    def out_places(n, s, g, count, stayed):
        return outs[:, bass.ds(G * (1 + RING * n + s) + g - (0 if stayed else G * RING * ROUNDS), count)]

    ROW_BANKS = 6
    assert 2 * E - ROW_BANKS <= E

    def row_ps(n):
        k = n % ROW_BANKS
        return out_ps[:, k] if k < 2 else z_ps[:, (k - 2) // 2, k % 2]

    with nc.Block() as block:

        @block.sync
        def _(sp):
            def body(i, stays):
                for token, g, group in tokens("sp", SP_ORDER, i):
                    if token == "X" and not (isinstance(group, int) and group == 0):
                        wait(sp, h2_ready, G * (group - 1) + 2 * g + 2)
                        sp.dma_start(x1_in[:, 2 * g:2 * g + 2], x1_dram[bass.ds(G * group + 2 * g, 2)].rearrange("g n f -> n g f")).then_inc(x1_loaded[g], 16)
                    elif token == "J":
                        wait(sp, adj_transposed, group)
                        sp.dma_start(adj_in2[:], adj[bass.ds(G * group, G)].rearrange("g n m -> n g m")).then_inc(adj2_loaded, 16)
                        if isinstance(group, int) and group == 0:
                            for dst, src in ((rw, router_w), (rb, router_b), (gamma_sb, gamma), (beta_sb, beta)):
                                sp.dma_start(dst[:], src).then_inc(const_loaded, 16)
                    elif token == "P" and not stays:
                        wait(sp, out_copied, G * group + g + 1)
                        sp.dma_start(out_dram[bass.ds(G * group + g, 1)].rearrange("g n f -> n (g f)"), outs[:, g]).then_inc(out_stored[g], 16)

            run(sp, body)

            sp.wait_ge(out_made, B)
            for g in range(G):
                sp.wait_ge(out_stored[g], 16 * STORED)

            def load_x1(n, s):
                stayed = n < ROUNDS
                if not stayed:
                    sp.wait_ge(y_ready, G * (RING * (n - ROUNDS) + s + 1))
                wait(sp, x1_chunk_loaded[s], 16 * n)
                sp.dma_start(x1_chunk(n, s, stayed).rearrange("p a g f -> p (a g) f"),
                             x1_dram[bass.ds(graph_of(n, s, 0, stayed), G)].rearrange("g n f -> n g f")).then_inc(x1_chunk_loaded[s], 16)

            def load_out(n, s):
                sp.wait_ge(y_stored[RING * (n - ROUNDS) + s], 16)
                wait(sp, out_chunk_loaded[s], 16 * (n - ROUNDS))
                sp.dma_start(out_places(n, s, 0, G, False),
                             out_dram[bass.ds(graph_of(n, s, 0, False), G)].rearrange("g n f -> n g f")).then_inc(out_chunk_loaded[s], 16)

            for n in range(CHUNKS // RING):
                for s in range(RING):
                    load_x1(n, s)
                    if n >= ROUNDS:
                        load_out(n, s)
            for stored in y_stored:
                sp.wait_ge(stored, 16 * 2)

        @block.gpsimd
        def _(pool):
            nc.gpsimd.memset(minus_half[:], -0.5)
            nc.gpsimd.memset(ones[:], 1.0)
            for e in range(E):
                nc.gpsimd.memset(expert_less_e[:, e:e + 1], float(e - E))
            nc.gpsimd.memset(adjT[:, :, N:N + 1], 1.0 / N).then_inc(consts, 1)

            def body(i, stays):
                for token, g, group in tokens("pool", POOL_ORDER, i):
                    if token == "N":
                        if isinstance(group, int) and group == 0 and g == 0:
                            pool.wait_ge(consts, 1)
                        half = slice(2 * g, 2 * g + 2)
                        wait(pool, var_ready, 2 * group + g + 1)
                        wait(pool, h2_ready, G * (group - 1) + 2 * g + 2)
                        nc.gpsimd.tensor_tensor(rstd[:, half], var_eps[:, half], minus_half[:, half], ALU.pow).then_inc(rstd_ready, 1)
                        wait(pool, rstd_ready, 2 * group + g + 1)
                        nc.gpsimd.tensor_tensor(shift[:, half], neg_mean[:, half], rstd[:, half], ALU.mult).then_inc(shift_ready, 1)
                        if isinstance(group, int) and group == 0 and g == 1:
                            nc.gpsimd.memset(sums[:], 0.0).then_inc(consts, 1)
                            pool.wait_ge(consts, 2)
                    elif token == "P":
                        n = G * group + g
                        if g == 0:
                            wait(pool, routed, group + 1)
                        e = pool.value_load(top1[0:1, bass.ds(n, 1)], min_val=0, max_val=E - 1)
                        wait(pool, out_copied, n + 1)
                        wait(pool, summed, n)
                        total = sums[:, 0, bass.ds(e, 1)].rearrange("p a f -> p (a f)")
                        nc.gpsimd.tensor_tensor(total, total, out_of(group, g, stays), ALU.add).then_inc(summed, 1)

            run(pool, body)
            pool.wait_ge(var_all_ready, 1)
            nc.gpsimd.tensor_tensor(inv_std[:].rearrange("p e c -> p (e c)"), var[:].rearrange("p e c -> p (e c)"),
                                    minus_half[:], ALU.pow).then_inc(inv_std_ready, 1)
            pool.wait_ge(rows_ready[1], E)

            def round_of(n, stayed):
                for s in range(RING):
                    for g in range(G):
                        e = pool.value_load(top1[0:1, bass.ds(graph_of(n, s, g, stayed), 1)], min_val=0, max_val=E - 1)
                        pool.wait_ge(scaled, G * (RING * n + s) + g + 1)
                        out = out_places(n, s, g, 1, stayed)
                        nc.gpsimd.tensor_tensor(out, out, coef_rows[1][:, bass.ds(e, 1)], ALU.add).then_inc(shifted, 1)

            for_rounds(pool, round_of)

        @block.scalar
        def _(act):
            def body(i, stays):
                for token, g, group in tokens("act", ACT_ORDER, i):
                    n = G * group + g
                    if token == "U":
                        act.wait_ge(w_raw_loaded[g], 16)
                        nc.scalar.activation(ew_hi[:, g], w_raw[:, g].bitcast(F32), ACT.Copy).then_inc(ew_hi_ready, 1)
                    elif token == "A":
                        wait(act, shift_ready, 2 * group + g // 2 + 1)
                        wait(act, z_made, n - G + 1)
                        nc.scalar.activation(h2[:, g], x1_in[:, g], ACT.Relu, bias=shift[:, g:g + 1],
                                             scale=rstd[:, g:g + 1]).then_inc(h2_ready, 1)
                    elif token == "P":
                        wait(act, out_made, n + 1)
                        if not stays:
                            wait(act, out_stored[g], 16 * group)
                        wait(act, summed, n - G + 1)
                        wait(act, square_summed, n - G + 1)
                        nc.scalar.activation(out_of(group, g, stays), out_ps[:, g % 2], ACT.Copy).then_inc(out_copied, 1)
                        nc.scalar.activation(square[:, g], out_ps[:, g % 2], ACT.Square).then_inc(squared, 1)
                    elif token == "Z":
                        wait(act, mean_ready, n + 1)
                        wait(act, out_made, n - G + 1)
                        nc.scalar.activation(z_hi[:, g].rearrange("p (a b) n -> p a b n", a=2),
                                             z_ps[:, g % 2, :, 0:2 * (N + 1)].rearrange("p a (b n) -> p a b n", b=2)[:, :, :, 0:N],
                                             ACT.Copy).then_inc(z_hi_ready, 1)

            run(act, body)
            for n in range(E, 2 * E):
                act.wait_ge(rows_made, n + 1)
                nc.scalar.activation(coef_rows[1][:, n - E], row_ps(n), ACT.Copy).then_inc(rows_ready[1], 1)

            for n in range(CHUNKS // RING):
                for s in range(RING):
                    stayed = n < ROUNDS
                    act.wait_ge(y_ready, G * (RING * n + s + 1))
                    act.dma_start(y[bass.ds(graph_of(n, s, 0, stayed), G)].rearrange("g n f -> n g f"),
                                  out_places(n, s, 0, G, stayed)).then_inc(y_stored[RING * (n % ROUNDS) + s], 16)

        @block.vector
        def _(dve):
            steps = 0

            def then_wait(instruction):
                nonlocal steps
                steps += 1
                instruction.then_inc(moment_step, 1)
                dve.wait_ge(moment_step, steps)

            def count_rows():
                dve.wait_ge(routed, GROUPS)
                for e in range(E):
                    nc.vector.tensor_scalar(is_expert[:, e], top1[:], float(e), None, ALU.is_equal).then_inc(counted, 1)
                dve.wait_ge(counted, E)
                then_wait(nc.vector.tensor_reduce(count[:], is_expert[:], X, ALU.add))
                then_wait(nc.vector.tensor_scalar(count[:], count[:], float(N), 1.0, ALU.mult, ALU.max))
                nc.vector.reciprocal(inv_count1[:], count[:]).then_inc(count_ready, 1)

            def body(i, stays):
                for token, g, group in tokens("dve", DVE_ORDER, i):
                    n = G * group + g
                    z = z_ps[:, g % 2, :, 0:2 * (N + 1)].rearrange("p a (b n) -> p a b n", b=2)
                    if token == "U":
                        dve.wait_ge(ew_hi_ready, g + 1)
                        nc.vector.tensor_tensor(ew_lo[:, g], w_raw[:, g].bitcast(F32), ew_hi[:, g], ALU.subtract).then_inc(ew_split, 1)
                    elif token == "N":
                        count_to = 2 * group + g + 1
                        half = slice(2 * g, 2 * g + 2)
                        of_half = [t[:, half] for t in (bn, mean_sum, mean_diff, m2)]
                        wait(dve, x1_loaded[g], 16 * (group + 1))
                        for place in range(2 * g, 2 * g + 2):
                            last = nc.vector.bn_stats(bn[:, place], x1_in[:, place])
                        last.then_inc(bn_done, 1)
                        wait(dve, bn_done, count_to)
                        halves_combined(nc, *of_half).then_inc(halves_done, 1)
                        wait(dve, halves_done, count_to)
                        wait(dve, shift_ready, count_to - 2)
                        scaled_moments(nc, D, *of_half[1:], neg_mean[:, half]).then_inc(scaled_done, 1)
                        wait(dve, scaled_done, count_to)
                        nc.vector.scalar_tensor_tensor(out=var_eps[:, half], in0=mean_diff[:, half], scalar=0.25,
                                                       in1=m2[:, half], op0=ALU.mult, op1=ALU.add).then_inc(var_ready, 1)
                    elif token == "S":
                        if isinstance(n, int) and n == B - G:
                            count_rows()
                        if g == 0 and isinstance(group, int):
                            dve.wait_ge(routed, group + 1)
                        e = dve.value_load(top1[0:1, bass.ds(n, 1)], min_val=0, max_val=E - 1)
                        wait(dve, squared, n + 1)
                        wait(dve, square_summed, n)
                        total = sums[:, 1, bass.ds(e, 1)].rearrange("p a f -> p (a f)")
                        nc.vector.tensor_tensor(total, total, square[:, g], ALU.add).then_inc(square_summed, 1)
                    elif token == "J":
                        wait(dve, adj_transposed, group + 1)
                        wait(dve, z_made, G * group)
                        nc.vector.tensor_copy(adjT[:, :, 0:N], adjT_ps[:]).then_inc(adjT_ready, 1)
                    elif token == "Y":
                        wait(dve, z_made, n + 1)
                        wait(dve, router_scored, group)
                        if g == 0:
                            wait(dve, routed, group)
                        nc.vector.tensor_copy(mean_h[:, g].rearrange("p (a b) -> p a b", a=2), z[:, :, :, N]).then_inc(mean_ready, 1)
                    elif token == "Z":
                        wait(dve, z_hi_ready, n + 1)
                        nc.vector.tensor_tensor(z_lo[:, g].rearrange("p (a b) n -> p a b n", a=2), z[:, :, :, 0:N],
                                                z_hi[:, g].rearrange("p (a b) n -> p a b n", a=2),
                                                ALU.subtract).then_inc(z_split, 1)
                    elif token == "M":
                        if isinstance(group, int) and group == 0:
                            dve.wait_ge(consts, 2)
                            dve.wait_ge(const_loaded, 64)
                        wait(dve, router_scored, group + 1)
                        nc.vector.tensor_tensor(score[:], router_ps[0:1, 0:G * E].rearrange("p (g e) -> p g e", g=G),
                                                rb[:].unsqueeze(1).to_broadcast([1, G, E]), ALU.add).then_inc(router_step, 1)
                        wait(dve, router_step, 4 * group + 1)
                        nc.vector.tensor_reduce(score_max[:], score[:], X, ALU.max).then_inc(router_step, 1)
                        wait(dve, router_step, 4 * group + 2)
                        nc.vector.tensor_tensor(best[:], score[:], score_max[:].unsqueeze(2).to_broadcast([1, G, E]),
                                                ALU.is_ge).then_inc(router_step, 1)
                        wait(dve, router_step, 4 * group + 3)
                        nc.vector.tensor_tensor(candidate[:], best[:], expert_less_e[:].unsqueeze(1).to_broadcast([1, G, E]),
                                                ALU.mult).then_inc(router_step, 1)
                        wait(dve, router_step, 4 * group + 4)
                        nc.vector.tensor_reduce(first[:], candidate[:], X, ALU.min).then_inc(first_ready, 1)
                        wait(dve, first_ready, group + 1)
                        nc.vector.tensor_scalar(top1[:, bass.ds(G * group, G)], first[:], float(E), float(E - 1), ALU.add,
                                                ALU.min).then_inc(routed, 1)

            run(dve, body)

            dve.wait_ge(inv_count_made, 1)
            then_wait(nc.vector.tensor_copy(inv_count[:], router_ps[:, 0:E]))
            for n in range(2 * E):
                dve.wait_ge(sums_transposed, n + 1)
                nc.vector.tensor_reduce(moment[:, n // E, n % E], row_ps(n).rearrange("p (c n) -> p c n", n=N), X,
                                        ALU.add).then_inc(moment_summed, 1)
            dve.wait_ge(moment_summed, 2 * E)
            for t in range(2):
                last = nc.vector.tensor_tensor(moment[:, t], moment[:, t], inv_count[:].unsqueeze(2).to_broadcast([128, E, KC]),
                                               ALU.mult)
            then_wait(last)
            then_wait(nc.vector.tensor_tensor(mean_sq[:], moment[:, 0], moment[:, 0], ALU.mult))
            then_wait(nc.vector.tensor_tensor(var[:], moment[:, 1], mean_sq[:], ALU.subtract))
            nc.vector.tensor_scalar(var[:], var[:], EPS, None, ALU.add).then_inc(var_all_ready, 1)
            dve.wait_ge(inv_std_ready, 1)
            then_wait(nc.vector.tensor_tensor(coef[:, 0], inv_std[:], gamma_sb[:], ALU.mult))
            then_wait(nc.vector.tensor_tensor(mean_sq[:], moment[:, 0], coef[:, 0], ALU.mult))
            nc.vector.tensor_tensor(coef[:, 1], beta_sb[:], mean_sq[:], ALU.subtract).then_inc(coef_ready, 1)
            for n in range(E):
                dve.wait_ge(rows_made, n + 1)
                nc.vector.tensor_copy(coef_rows[0][:, n], row_ps(n)).then_inc(rows_ready[0], 1)
            dve.wait_ge(rows_ready[0], E)

            LAG = 2

            def round_of(n, stayed):
                for k in range(RING * G + LAG):
                    if k < RING * G:
                        s, g = k // G, k % G
                        e = dve.value_load(top1[0:1, bass.ds(graph_of(n, s, g, stayed), 1)], min_val=0, max_val=E - 1)
                        if g == 0 and not stayed:
                            dve.wait_ge(out_chunk_loaded[s], 16 * (n - ROUNDS + 1))
                        out = out_places(n, s, g, 1, stayed)
                        nc.vector.tensor_tensor(out, out, coef_rows[0][:, bass.ds(e, 1)], ALU.mult).then_inc(scaled, 1)
                    if k >= LAG:
                        s, g = (k - LAG) // G, (k - LAG) % G
                        dve.wait_ge(shifted, RING * G * n + k - LAG + 1)
                        if g == 0:
                            dve.wait_ge(x1_chunk_loaded[s], 16 * (n + 1))
                        out = out_places(n, s, g, 1, stayed)
                        nc.vector.scalar_tensor_tensor(out=out, in0=out, scalar=0.0, in1=x1_chunk(n, s, stayed)[:, :, g],
                                                       op0=ALU.max, op1=ALU.add).then_inc(y_ready, 1)

            for_rounds(dve, round_of)

        @block.tensor
        def _(pe):
            def body(i, stays):
                for token, g, group in tokens("pe", PE_ORDER, i):
                    n = G * group + g
                    if token == "J":
                        wait(pe, adj2_loaded, 16 * (group + 1))
                        wait(pe, adjT_ready, group)
                        for k in range(G):
                            last = nc.tensor.transpose(adjT_ps[:, k], adj_in2[:, k], ident[:])
                        last.then_inc(adj_transposed, 1)
                    elif token == "Z":
                        if isinstance(n, int) and n == 0:
                            pe.wait_ge(consts, 1)
                            pe.wait_ge(const_loaded, 64)
                        wait(pe, h2_ready, n + 1)
                        wait(pe, adjT_ready, group + 1)
                        wait(pe, z_split, n - 1)
                        wait(pe, mean_ready, n - 1)
                        for c in range(KC):
                            at = (c % 2) * (N + 1)
                            last = nc.tensor.matmul(z_ps[:, g % 2, c // 2, at:at + N + 1], h2[:, g, 128 * c:128 * c + 128],
                                                    adjT[:, g], start=True, stop=True)
                        last.then_inc(z_made, 1)
                    elif token == "M":
                        wait(pe, mean_ready, G * (group + 1))
                        wait(pe, routed, group)
                        for k in range(G):
                            for c in range(KC):
                                last = nc.tensor.matmul(router_ps[0:1, E * k:E * k + E], mean_h[:, k, c:c + 1], rw[:, c],
                                                        start=(c == 0), stop=(c == KC - 1))
                        last.then_inc(router_scored, 1)
                    elif token == "P":
                        if isinstance(n, int) and n == 0:
                            pe.wait_ge(ew_split, E)
                        if g == 0:
                            wait(pe, routed, group + 1)
                        e = pe.value_load(top1[0:1, bass.ds(n, 1)], min_val=0, max_val=E - 1)
                        wait(pe, z_split, n + 1)
                        wait(pe, squared, n - 1)

                        def of_expert(w, c):
                            return w[:, bass.ds(e, 1), c].rearrange("p a f -> p (a f)")

                        exact_product(nc, out_ps[:, g % 2], [z_hi[:, g, c] for c in range(KC)], [z_lo[:, g, c] for c in range(KC)],
                                      [of_expert(ew_hi, c) for c in range(KC)], [of_expert(ew_lo, c) for c in range(KC)]
                                      ).then_inc(out_made, 1)

            keep_clock_up(nc, pe, adjT_ps[:, 0], ident, 16)
            run(pe, body)

            pe.wait_ge(summed, B)
            pe.wait_ge(square_summed, B)
            pe.wait_ge(count_ready, 1)
            nc.tensor.matmul(router_ps[:, 0:E], ones[0:1, :], inv_count1[:], start=True, stop=True).then_inc(inv_count_made, 1)
            for n in range(2 * E):
                if n >= ROW_BANKS:
                    pe.wait_ge(moment_summed, n - ROW_BANKS + 1)
                for c in range(KC):
                    last = nc.tensor.transpose(row_ps(n)[:, 128 * c:128 * c + 128],
                                               sums[:, n // E, n % E, 128 * c:128 * c + 128], ident[:])
                last.then_inc(sums_transposed, 1)
            keep_clock_up(nc, pe, adjT_ps[:, 0], ident, 56)
            pe.wait_ge(coef_ready, 1)
            for n in range(2 * E):
                if n >= ROW_BANKS:
                    pe.wait_ge(rows_ready[0], n - ROW_BANKS + 1)
                for c in range(KC):
                    last = nc.tensor.transpose(row_ps(n)[:, 128 * c:128 * c + 128],
                                               coef[:, n // E, n % E, c:c + 1].to_broadcast([128, 128]), ident[:])
                last.then_inc(rows_made, 1)


def program(nc, x, adj, wq, wk, wv, wo, router_w, router_b, expert_w, gamma, beta, y):
    B, N, D = x.shape
    x1_dram = nc.dram_tensor("x1_dram", [B, N, D], F32, kind="Internal").ap()
    out_dram = nc.dram_tensor("out_dram", [B, N, D], F32, kind="Internal").ap()
    with ExitStack() as outer:
        def sem(name):
            return outer.enter_context(nc.semaphore(name))

        ident = outer.enter_context(nc.sbuf_tensor("ident", [128, 128], F32))
        ident_step = sem("ident_step")
        with nc.Block() as block:

            @block.gpsimd
            def _(pool):
                nc.gpsimd.memset(ident[:], 0.0).then_inc(ident_step, 1)
                pool.wait_ge(ident_step, 1)
                nc.gpsimd.affine_select(out=ident[:], in_=ident[:], compare_op=ALU.not_equal, fill=1.0, base=0,
                                        pattern=[[-1, 128]], channel_multiplier=1).then_inc(ident_step, 1)
                pool.wait_ge(ident_step, 2)

        E, D = expert_w.shape[0:2]
        w_hi = outer.enter_context(nc.sbuf_tensor("w_hi", [128, 4, D // 128, D], F32R))
        w_raw = outer.enter_context(nc.sbuf_tensor("expert_w_raw", [128, E, D // 128, D], F32R))
        x1_in = outer.enter_context(nc.sbuf_tensor("x1_in", [N, 4, D], F32))
        shared = (w_hi, w_raw, [sem(f"w_raw_loaded{e}") for e in range(E)], sem("ew_hi_ready"), sem("ew_split"),
                  x1_in, [sem("x1_loaded0"), sem("x1_loaded1")])
        with ExitStack() as ctx:
            attention_layer(nc, ctx, sem, ident, x, adj, (wq, wk, wv, wo), x1_dram, expert_w, shared)
        with ExitStack() as ctx:
            expert_layer(nc, ctx, sem, ident, x1_dram, adj, router_w, router_b, gamma, beta, out_dram, y, shared)


def kernel(x, adj, L0_gnn_Wq, L0_gnn_Wk, L0_gnn_Wv, L0_gnn_Wo, L1_gnn_router_w, L1_gnn_router_b, L1_gnn_expert_w,
           L1_gnn_bn_gamma, L1_gnn_bn_beta):
    import numpy as np
    import concourse.bacc as bacc
    from concourse.bass_utils import run_bass_kernel_spmd

    E, D = np.shape(L1_gnn_bn_gamma)
    C = D // 128

    def by_feature(a):
        return np.asarray(a).reshape(E, C, 128).transpose(2, 0, 1)

    inputs = {
        "x": x,
        "adj": adj,
        "wq": np.asarray(L0_gnn_Wq).T,
        "wk": np.asarray(L0_gnn_Wk).T,
        "wv": np.asarray(L0_gnn_Wv).T,
        "wo": np.asarray(L0_gnn_Wo).T,
        "router_w": np.asarray(L1_gnn_router_w).reshape(C, 128, E).transpose(1, 0, 2),
        "router_b": np.asarray(L1_gnn_router_b).reshape(1, E),
        "expert_w": L1_gnn_expert_w,
        "gamma": by_feature(L1_gnn_bn_gamma),
        "beta": by_feature(L1_gnn_bn_beta),
    }
    arrays = {f"in_{name}": np.ascontiguousarray(a) for name, a in inputs.items()}
    nc = bacc.Bacc("TRN2", target_bir_lowering=False, num_devices=1)
    args = [nc.dram_tensor(name, a.shape, mybir.dt.from_np(a.dtype), kind="ExternalInput").ap() for name, a in arrays.items()]
    y = nc.dram_tensor("y", np.shape(x), F32, kind="ExternalOutput").ap()
    program(nc, *args, y)
    return run_bass_kernel_spmd(nc, [arrays], core_ids=[0]).results[0]["y"]
```
